# Optimizing a Trainium2 kernel written in Bass

```python
import numpy as np
import jax
import jax.numpy as jnp

def _softmax(x, axis=-1):
    return jax.nn.softmax(x, axis=axis)

def _gelu(x):
    return jax.nn.gelu(x, approximate=True)

def _silu(x):
    return jax.nn.silu(x)

def _sigmoid(x):
    return jax.nn.sigmoid(x)

def _layernorm(x, axis=-1, eps=1e-05):
    m = jnp.mean(x, axis=axis, keepdims=True)
    v = jnp.var(x, axis=axis, keepdims=True)
    return (x - m) / jnp.sqrt(v + eps)

def _scatter_add(tgt, idx, src, axis=0):
    return tgt.at[idx].add(src)

def _segment_sum(src, seg, n):
    return jax.ops.segment_sum(src, seg, n)
kernel_name = 'mk_seq_preln_d1_jaxref_r8_8887c0'

def setup_inputs(seed: int=0):
    np.random.seed(seed)
    _w = jnp.asarray

    def _L0_attn_setup():
        import jax, jax.numpy as jnp
        import numpy as np
        B, S, D = (4, 256, 128)
        SCALE = 1.0 / np.sqrt(D)
        key = jax.random.key(seed)
        k1, k2, k3 = jax.random.split(key, 3)
        x = jax.random.normal(k1, (B, S, D), dtype=jnp.float32)
        bound = 1.0 / np.sqrt(D)
        W_qk = jax.random.uniform(k2, (D, D), minval=-bound, maxval=bound, dtype=jnp.float32)
        W_v = jax.random.uniform(k3, (D, D), minval=-bound, maxval=bound, dtype=jnp.float32)
        alibi_slope = jnp.full((1,), 0.5, dtype=jnp.float32)
        return {'x': x, 'W_qk': W_qk, 'W_v': W_v, 'alibi_slope': alibi_slope}
    _L0_attn_in = _L0_attn_setup()

    def _L0_ffn_setup():
        import jax, jax.numpy as jnp
        import numpy as np
        DIM = 128
        HIDDEN = 384
        SCALE = 1.0 / 127.0

        def _dequant(w_int, dtype):
            return w_int.astype(dtype) * jnp.asarray(SCALE, dtype)
        key = jax.random.key(seed)
        k_x, k_g, k_u, k_d = jax.random.split(key, 4)
        x = jax.random.normal(k_x, (4, 256, DIM), dtype=jnp.float32)
        w_gate = jax.random.randint(k_g, (HIDDEN, DIM), -127, 128, dtype=jnp.int32)
        w_up = jax.random.randint(k_u, (HIDDEN, DIM), -127, 128, dtype=jnp.int32)
        w_down = jax.random.randint(k_d, (DIM, HIDDEN), -127, 128, dtype=jnp.int32)
        return {'x': x, 'w_gate': w_gate, 'w_up': w_up, 'w_down': w_down}
    _L0_ffn_in = _L0_ffn_setup()
    _d = {'L0_attn_x': _L0_attn_in['x'], 'L0_attn_W_qk': _L0_attn_in['W_qk'], 'L0_attn_W_v': _L0_attn_in['W_v'], 'L0_attn_alibi_slope': _L0_attn_in['alibi_slope'], 'L0_ffn_w_gate': _L0_ffn_in['w_gate'], 'L0_ffn_w_up': _L0_ffn_in['w_up'], 'L0_ffn_w_down': _L0_ffn_in['w_down']}
    _x0 = _d['L0_attn_x']
    _d['L0_attn_x'] = jax.random.normal(jax.random.fold_in(jax.random.key(seed), 1), (4, 1024, 128), dtype=_x0.dtype)
    del _x0
    return _d

def reference(L0_attn_x, L0_attn_W_qk, L0_attn_W_v, L0_attn_alibi_slope, L0_ffn_w_gate, L0_ffn_w_up, L0_ffn_w_down):

    def _L0_attn_ref(x, W_qk, W_v, alibi_slope):
        import jax, jax.numpy as jnp
        import numpy as np
        B, S, D = (4, 256, 128)
        SCALE = 1.0 / np.sqrt(D)
        seq_len = x.shape[1]
        scores = jnp.einsum('bqe,bke->bqk', x @ W_qk, x) * SCALE
        kpos = jnp.arange(seq_len, dtype=x.dtype)[None, :]
        qpos = jnp.arange(seq_len, dtype=x.dtype)[:, None]
        scores = scores + (kpos - qpos) * alibi_slope[0]
        causal = qpos >= kpos
        scores = jnp.where(causal, scores, -jnp.inf)
        attn = jax.nn.softmax(scores, axis=-1)
        v = x @ W_v.T
        return jnp.einsum('bqk,bkd->bqd', attn, v)

    def _L0_ffn_ref(x, w_gate, w_up, w_down):
        import jax, jax.numpy as jnp
        import numpy as np
        DIM = 128
        HIDDEN = 384
        SCALE = 1.0 / 127.0

        def _dequant(w_int, dtype):
            return w_int.astype(dtype) * jnp.asarray(SCALE, dtype)
        wg = _dequant(w_gate, x.dtype)
        wu = _dequant(w_up, x.dtype)
        wd = _dequant(w_down, x.dtype)
        gate = jnp.einsum('bsd,hd->bsh', x, wg)
        up = jnp.einsum('bsd,hd->bsh', x, wu)
        h = jax.nn.silu(gate) * up
        return jnp.einsum('bsh,dh->bsd', h, wd)
    x = L0_attn_x
    x = x + _L0_attn_ref(_layernorm(x, axis=-1), L0_attn_W_qk, L0_attn_W_v, L0_attn_alibi_slope)
    x = x + _L0_ffn_ref(_layernorm(x, axis=-1), L0_ffn_w_gate, L0_ffn_w_up, L0_ffn_w_down)
    return x

_drawn_inputs = setup_inputs


def setup_inputs(seed=0):
    import zlib

    import numpy as np

    out = dict(_drawn_inputs(seed))
    spreads = {}
    factors = {}
    for name, (base, spread) in spreads.items():
        noise = np.random.default_rng([zlib.crc32(name.encode()), seed]).standard_normal(out[name].shape)
        drawn = base * np.exp(spread * noise) if base else spread * noise
        out[name] = jnp.asarray(drawn.astype(out[name].dtype))
    for name, factor in factors.items():
        out[name] = (out[name] * factor).astype(out[name].dtype)
    return out
```

```python
from contextlib import ExitStack

import concourse.bass as bass
from concourse import mybir

ALU = mybir.AluOpType
ACT = mybir.ActivationFunctionType
F32 = mybir.dt.float32
F16 = mybir.dt.float16
I32 = mybir.dt.int32
U32 = mybir.dt.uint32
AX_X = mybir.AxisListType.X
ds = bass.ds

P = 128
EPS = 1e-5
DEQUANT = 1.0 / 127.0
EXPONENT_BITS = 0x7F800000
F16_EXACT = 1024.0
MASKED = -3.0e38


def preln_block(nc, x, w_qk, w_v, slope, w_gate, w_up, w_down, out):
    B, S, D = x.shape
    HID = w_gate.shape[0]
    TB = S // P
    NT = B * TB
    HB = HID // P
    CT = 4
    CW = CT * P
    NCH = NT // CT
    HALVES = S // CW
    SCALE = float(D) ** -0.5
    assert D == P and S == 2 * CW and HID % P == 0

    NWORK = 3
    prologue = [(kind, h) for kind in ("xT", "q", "v") for h in range(HALVES)]
    steps = []
    for i in range(TB):
        steps += [(i, h) for h in range(i // CT + 1)]
        if 1 <= i <= len(prologue):
            steps.append(prologue[i - 1])
    first = {g: n for n, g in enumerate(prologue)}
    later = {g: n for n, g in enumerate(steps)}
    last = {g: n for n, g in enumerate([g for g in steps if g not in first])}
    PRO, PER = len(prologue), len(steps)
    assert PER % NWORK == 0 and PRO % NWORK == 0

    def bank_use(b, group, ahead=False):
        if ahead and isinstance(b, int) and b == 0:
            n = first[group]
            return n % NWORK, n // NWORK
        if ahead:
            n = later[group]
            return n % NWORK, (b - 1) * (PER // NWORK) + (PRO + n) // NWORK
        n = last[group] if isinstance(b, int) and b == B - 1 else later[group]
        return n % NWORK, b * (PER // NWORK) + (PRO + n) // NWORK

    WORK_USES = [(PRO + PER * (B - 1) + len(last)) // NWORK] * NWORK
    assert len(last) % NWORK == 0

    with ExitStack() as ctx:
        def sb(name, shape, dt):
            return ctx.enter_context(nc.sbuf_tensor(name, shape, dt))

        def sem(name):
            return ctx.enter_context(nc.semaphore(name))

        wqk_in = sb("wqk_in", [P, D], F32)
        wv_in = sb("wv_in", [P, D], F32)
        wgu_int = sb("wgu_int", [P, 2 * HB, D], I32)
        wd_int = sb("wd_int", [P, HID], I32)
        wgu_in = sb("wgu_in", [P, 2 * HB, D], F32)
        wd_in = sb("wd_in", [P, HID], F32)
        slope_col = sb("slope_col", [P, 1], F32)
        ident = sb("ident", [P, P], F32)
        ones4 = sb("ones4", [4, P], F32)
        wmax = sb("wmax", [P, 4], F32)
        wmax_row = sb("wmax_row", [4, 1], F32)
        wpow_row = sb("wpow_row", [4, 1], F32)
        wpow_diag = sb("wpow_diag", [4, 4], F32)
        wpow = sb("wpow", [P, 4], F32)
        wpow_inv = sb("wpow_inv", [P, 4], F32)
        gu_scale = sb("gu_scale", [P, 1], F32)
        gu_unscale = sb("gu_unscale", [P, 1], F32)
        gate_scale = sb("gate_scale", [P, 1], F32)
        ffn_scale = sb("ffn_scale", [P, 1], F32)
        score_scale = sb("score_scale", [P, 1], F32)
        neg_score_scale = sb("neg_score_scale", [P, 1], F32)
        score_inv = sb("score_inv", [P, 1], F32)
        slope_scaled = sb("slope_scaled", [P, 1], F32)
        distance = sb("distance", [P, S], F32)
        bias_raw = sb("bias_raw", [P, S], F32)
        bias = sb("bias", [P, S], F32)
        wtmp = sb("wtmp", [P, 2, D], F32)
        wqk = sb("wqk", [P, 2, D], F16)
        wvT = sb("wvT", [P, 2, D], F16)
        wguT_f = sb("wguT_f", [P, 2 * HB, P], F32)
        wguT = sb("wguT", [P, 2, 2 * HB, P], F16)
        wdT = sb("wdT", [P, HB, D], F32)
        norm_const = sb("norm_const", [P, 5], F32)

        xs = sb("xs", [P, NT, D], F32)
        stats = sb("stats", [P, TB, 6], F32)
        mean_sum = sb("mean_sum", [P, TB], F32)
        mean_dif = sb("mean_dif", [P, TB], F32)
        dif_sq = sb("dif_sq", [P, TB], F32)
        square_sum = sb("square_sum", [P, TB], F32)
        between = sb("between", [P, TB], F32)
        within = sb("within", [P, TB], F32)
        within_eps = sb("within_eps", [P, TB], F32)
        mean = sb("mean", [P, TB], F32)
        var_eps = sb("var_eps", [P, TB], F32)
        rstd = sb("rstd", [P, TB], F32)
        centred = sb("centred", [P, TB, D], F32)
        xn = sb("xn", [P, TB, D], F32)
        xT_hi = sb("xT_hi", [P, 2, S], F16)
        xT_lo = sb("xT_lo", [P, 2, S], F16)
        qT_hi = sb("qT_hi", [P, 2, S], F16)
        qT_lo = sb("qT_lo", [P, 2, S], F16)
        v = sb("v", [P, 2, S], F32)
        biased = sb("biased", [P, 2, S], F32)
        probs = sb("probs", [P, 2, S], F32)
        probsT = sb("probsT", [P, 2, S], F32)
        neg_max = sb("neg_max", [P, TB], F32)
        prob_sum = sb("prob_sum", [P, TB], F32)
        inv_sum = sb("inv_sum", [P, TB], F32)
        x2T_hi = sb("x2T_hi", [P, 2, CW], F16)
        x2T_lo = sb("x2T_lo", [P, 2, CW], F16)
        silu = sb("silu", [P, HB, CW], F32)
        hidden = sb("hidden", [P, HB, CW], F32)

        score_ps = ctx.enter_context(nc.psum_tensor("score_ps", [P, 2, S], F32))
        attn_ps = ctx.enter_context(nc.psum_tensor("attn_ps", [P, 512], F32))
        work_ps = ctx.enter_context(nc.psum_tensor("work_ps", [P, NWORK, 512], F32))
        gate_ps = [score_ps[:, 0, 0:CW], score_ps[:, 0, CW:S], score_ps[:, 1, 0:CW]]
        up_ps = [score_ps[:, 1, CW:S], work_ps[:, 0, :], work_ps[:, 1, :]]
        x2T_ps = work_ps[:, 2, :]
        down_ps = attn_ps[:, :]

        x_loaded = [sem(f"x_loaded{b}") for b in range(B)]
        w_loaded = sem("w_loaded")
        const_ready = sem("const_ready")
        ident_ready = sem("ident_ready")
        w_step = sem("w_step")
        w_max_ready = sem("w_max_ready")
        w_pe = sem("w_pe")
        w_ready = sem("w_ready")
        distance_ready = sem("distance_ready")
        bias_raw_ready = sem("bias_raw_ready")
        bias_ready = sem("bias_ready")
        stats_done = sem("stats_done")
        pool_step = sem("pool_step")
        xn_ready = sem("xn_ready")
        work_filled = [sem(f"work_filled{i}") for i in range(NWORK)]
        work_emptied = [sem(f"work_emptied{i}") for i in range(NWORK)]
        hi_ready = sem("hi_ready")
        scores_ready = sem("scores_ready")
        biased_ready = sem("biased_ready")
        probs_ready = sem("probs_ready")
        attn_ready = sem("attn_ready")
        inv_ready = sem("inv_ready")
        attn_added = sem("attn_added")
        x2T_filled = sem("x2T_filled")
        x2T_hi_ready = sem("x2T_hi_ready")
        x2T_ready = sem("x2T_ready")
        gate_up_ready = sem("gate_up_ready")
        silu_ready = sem("silu_ready")
        hidden_ready = sem("hidden_ready")
        down_ready = sem("down_ready")
        result_ready = sem("result_ready")
        stored = sem("stored")

        W_DIAG = 6
        N_SMALL = 10

        block = ctx.enter_context(nc.Block())

        @block.sync
        def _(sp):
            xv = x.rearrange("b (j p) d -> b p j d", p=P)
            ov = out.rearrange("b (j p) d -> p (b j) d", p=P)
            sp.dma_start(xs[:, 0:TB, :], xv[0]).then_inc(x_loaded[0], 16)
            sp.dma_start(wqk_in[:, :], w_qk).then_inc(w_loaded, 16)
            sp.dma_start(wv_in[:, :], w_v).then_inc(w_loaded, 16)
            sp.dma_start(wgu_int[:, 0:HB, :], w_gate.rearrange("(j p) d -> p j d", p=P)).then_inc(w_loaded, 16)
            sp.dma_start(wgu_int[:, HB:2 * HB, :], w_up.rearrange("(j p) d -> p j d", p=P)).then_inc(w_loaded, 16)
            sp.dma_start(wd_int[:, :], w_down).then_inc(w_loaded, 16)
            sp.dma_start(slope_col[:, :], slope.rearrange("(a d) -> a d", a=1).broadcast_to([P, 1])).then_inc(w_loaded, 16)
            for b in range(1, B):
                sp.dma_start(xs[:, TB * b:TB * (b + 1), :], xv[b]).then_inc(x_loaded[b], 16)
            with sp.Fori(0, NCH) as c:
                sp.wait_ge(result_ready, c + 1)
                sp.dma_start(ov[:, ds(CT * c, CT), :], xs[:, ds(CT * c, CT), :]).then_inc(stored, 16)
            sp.wait_ge(stored, 16 * NCH)

        @block.gpsimd
        def _(pool):
            pool.memset(ident[:, :], 0.0).then_inc(const_ready, 1)
            pool.memset(ones4[:, :], 1.0).then_inc(const_ready, 1)
            for n, value in enumerate((0.5, 0.25, 1.0 / D, EPS, -0.5)):
                pool.memset(norm_const[:, n:n + 1], value).then_inc(const_ready, 1)
            pool.wait_ge(const_ready, 7)
            pool.affine_select(out=ident[:, :], in_=ident[:, :], compare_op=ALU.not_equal, fill=1.0, base=0,
                               pattern=[[-1, P]], channel_multiplier=1).then_inc(ident_ready, 1)
            pool.iota(distance[:, :], pattern=[[1, S]], base=P - S, channel_multiplier=-1,
                      allow_small_or_imprecise_dtypes=True).then_inc(distance_ready, 1)

            def normalise(n, steps, nt, tiles, xn_used):
                half, quarter, per_element, eps, power = (norm_const[:, k:k + 1].broadcast_to([P, nt]) for k in range(5))

                def small(out, a, b, op):
                    pool.tensor_tensor(out[:, 0:nt], a, b, op).then_inc(pool_step, 1)

                pool.wait_ge(stats_done, n + 1)
                small(mean_sum, stats[:, 0:nt, 1], stats[:, 0:nt, 4], ALU.add)
                small(mean_dif, stats[:, 0:nt, 1], stats[:, 0:nt, 4], ALU.subtract)
                small(square_sum, stats[:, 0:nt, 2], stats[:, 0:nt, 5], ALU.add)
                pool.wait_ge(pool_step, steps + 3)
                small(mean, mean_sum[:, 0:nt], half, ALU.mult)
                small(dif_sq, mean_dif[:, 0:nt], mean_dif[:, 0:nt], ALU.mult)
                small(within, square_sum[:, 0:nt], per_element, ALU.mult)
                pool.wait_ge(pool_step, steps + 6)
                small(between, dif_sq[:, 0:nt], quarter, ALU.mult)
                small(within_eps, within[:, 0:nt], eps, ALU.add)
                pool.wait_ge(pool_step, steps + 8)
                small(var_eps, within_eps[:, 0:nt], between[:, 0:nt], ALU.add)
                pool.wait_ge(pool_step, steps + 9)
                small(rstd, var_eps[:, 0:nt], power, ALU.pow)
                for h in range(nt // CT):
                    t = slice(CT * h, CT * h + CT)
                    pool.tensor_tensor(centred[:, t, :], tiles(h),
                                       mean[:, t].rearrange("p (t a) -> p t a", a=1).broadcast_to([P, CT, D]),
                                       ALU.subtract).then_inc(pool_step, 1)
                    pool.wait_ge(pool_step, steps + N_SMALL + h + 1)
                    if h == 0:
                        xn_used()
                    pool.tensor_tensor(xn[:, t, :], centred[:, t, :],
                                       rstd[:, t].rearrange("p (t a) -> p t a", a=1).broadcast_to([P, CT, D]),
                                       ALU.mult).then_inc(xn_ready, 1)

            def attention_norm(b):
                def xn_used():
                    if isinstance(b, int) and b == 0:
                        return
                    for h in range(HALVES):
                        bank, used = bank_use(b - 1, ("xT", h), ahead=True)
                        pool.wait_ge(work_filled[bank], used + 1)

                normalise(b, (N_SMALL + HALVES) * b, TB, lambda h: xs[:, ds(TB * b + CT * h, CT), :], xn_used)

            def ffn_norm(c):
                def xn_used():
                    if isinstance(c, int) and c == 0:
                        for h in range(HALVES):
                            bank, used = bank_use(B - 1, ("xT", h), ahead=True)
                            pool.wait_ge(work_filled[bank], used + 1)
                    else:
                        pool.wait_ge(x2T_filled, c)

                normalise(B + c, (N_SMALL + HALVES) * B + (N_SMALL + 1) * c, CT, lambda h: xs[:, ds(CT * c, CT), :], xn_used)

            attention_norm(0)
            pool.wait_ge(bias_raw_ready, 1)
            pool.affine_select(out=bias[:, :], in_=bias_raw[:, :], compare_op=ALU.is_ge, fill=MASKED,
                               base=S - P, pattern=[[-1, S]], channel_multiplier=1).then_inc(bias_ready, 1)
            attention_norm(1)
            with pool.Fori(2, B) as b:
                attention_norm(b)
            ffn_norm(0)
            with pool.Fori(1, NCH) as c:
                ffn_norm(c)

        @block.tensor
        def _(pe):
            def transpose_weights():
                pe.wait_ge(ident_ready, 1)
                pe.wait_ge(w_max_ready, 1)
                pe.transpose(attn_ps[0:4, 0:P], wmax[:, :], ident[:, :]).then_inc(w_pe, 1)
                pe.transpose(work_ps[:, 0, 0:P], wv_in[:, :], ident[:, :])
                for j in range(HB):
                    pe.transpose(work_ps[:, 0, P * (j + 1):P * (j + 2)], wd_in[:, P * j:P * (j + 1)], ident[:, :])
                for j in range(2 * HB):
                    m = pe.transpose(score_ps[:, j // HB, P * (j % HB):P * (j % HB + 1)], wgu_in[:, j, :], ident[:, :])
                m.then_inc(w_pe, 1)
                pe.wait_ge(w_step, W_DIAG)
                pe.matmul(attn_ps[:, 256:260], ones4[:, :], wpow_diag[:, :], start=True, stop=True).then_inc(w_pe, 1)
                pe.wait_ge(w_ready, 1)

            def fill(b, group, ahead, emit):
                bank, used = bank_use(b, group, ahead)
                pe.wait_ge(work_emptied[bank], used)
                emit(work_ps[:, bank, :]).then_inc(work_filled[bank], 1)

            def taken(b, group, ahead):
                bank, used = bank_use(b, group, ahead)
                pe.wait_ge(work_emptied[bank], used + 1)

            def prologue_part(b, par, kind, h):
                cols = slice(CW * h, CW * h + CW)

                def transpose_x(ps):
                    for j in range(CT):
                        m = pe.transpose(ps[:, P * j:P * (j + 1)], xn[:, CT * h + j, :], ident[:, :])
                    return m

                def project_q(ps):
                    pe.matmul(ps, wqk[:, 0, :], xT_hi[:, ds(par, 1), cols].rearrange("p a n -> p (a n)"), start=True, stop=False)
                    pe.matmul(ps, wqk[:, 0, :], xT_lo[:, ds(par, 1), cols].rearrange("p a n -> p (a n)"), start=False, stop=False)
                    return pe.matmul(ps, wqk[:, 1, :], xT_hi[:, ds(par, 1), cols].rearrange("p a n -> p (a n)"), start=False, stop=True)

                def project_v(ps):
                    for j in range(CT):
                        tok = slice(CW * h + P * j, CW * h + P * j + P)
                        hi = xT_hi[:, ds(par, 1), tok].rearrange("p a n -> p (a n)")
                        lo = xT_lo[:, ds(par, 1), tok].rearrange("p a n -> p (a n)")
                        o = ps[:, P * j:P * j + P]
                        pe.matmul(o, hi, wvT[:, 0, :], start=True, stop=False)
                        pe.matmul(o, hi, wvT[:, 1, :], start=False, stop=False)
                        m = pe.matmul(o, lo, wvT[:, 0, :], start=False, stop=True)
                    return m

                if kind == "xT":
                    pe.wait_ge(xn_ready, HALVES * b + h + 1)
                    fill(b, (kind, h), True, transpose_x)
                else:
                    taken(b, ("xT", h), True)
                    fill(b, (kind, h), True, project_q if kind == "q" else project_v)

            def scores(b, par, i):
                t = TB * b + i
                if i % CT < 2:
                    taken(b, ("q", i // CT), True)
                if not (isinstance(b, int) and t < 2):
                    pe.wait_ge(biased_ready, t - 1)
                q_hi = qT_hi[:, ds(par, 1), P * i:P * (i + 1)].rearrange("p a n -> p (a n)")
                q_lo = qT_lo[:, ds(par, 1), P * i:P * (i + 1)].rearrange("p a n -> p (a n)")
                for k0 in range(0, P * (i + 1), CW):
                    n = min(CW, P * (i + 1) - k0)
                    k_hi = xT_hi[:, ds(par, 1), k0:k0 + n].rearrange("p a n -> p (a n)")
                    k_lo = xT_lo[:, ds(par, 1), k0:k0 + n].rearrange("p a n -> p (a n)")
                    o = score_ps[:, i % 2, k0:k0 + n]
                    pe.matmul(o, q_hi, k_hi, start=True, stop=False)
                    pe.matmul(o, q_hi, k_lo, start=False, stop=False)
                    m = pe.matmul(o, q_lo, k_hi, start=False, stop=True)
                m.then_inc(scores_ready, 1)

            def transpose_probs(b, i):
                pe.wait_ge(probs_ready, TB * b + i + 1)
                for h in range(i // CT + 1):
                    def emit(ps, h=h):
                        for j in range(min(CT, i + 1 - CT * h)):
                            k0 = CW * h + P * j
                            m = pe.transpose(ps[:, P * j:P * (j + 1)], probs[:, i % 2, k0:k0 + P], ident[:, :])
                        return m
                    fill(b, (i, h), False, emit)

            def weigh_values(b, par, i):
                if i < 1:
                    taken(b, ("v", 0), True)
                    taken(b, ("v", 1), True)
                pe.wait_ge(attn_added, TB * b + i)
                for h in range(i // CT + 1):
                    taken(b, (i, h), False)
                for j in range(i + 1):
                    m = pe.matmul(attn_ps[:, 0:D], probsT[:, i % 2, P * j:P * (j + 1)],
                                  v[:, ds(par, 1), P * j:P * (j + 1)].rearrange("p a n -> p (a n)"),
                                  start=(j == 0), stop=(j == i))
                m.then_inc(attn_ready, 1)

            def batch(b, par, nxt, final):
                for i in range(TB):
                    transpose_probs(b, i)
                    if not final and 1 <= i <= PRO:
                        prologue_part(b + 1, nxt, *prologue[i - 1])
                    if i + 2 < TB:
                        scores(b, par, i + 2)
                    elif not final:
                        scores(b + 1, nxt, i + 2 - TB)
                    weigh_values(b, par, i)

            transpose_weights()
            for part in prologue:
                prologue_part(0, 0, *part)
            pe.wait_ge(w_ready, 2)
            scores(0, 0, 0)
            scores(0, 0, 1)
            with pe.Fori(0, B - 1) as b:
                batch(b, pe.snap(b % 2), pe.snap((b + 1) % 2), False)
            batch(B - 1, (B - 1) % 2, B % 2, True)

            pe.wait_ge(biased_ready, NT)
            pe.wait_ge(attn_added, NT)
            for i in range(NWORK):
                pe.wait_ge(work_emptied[i], WORK_USES[i])

            def transpose_x2(c):
                pe.wait_ge(xn_ready, HALVES * B + c + 1)
                pe.wait_ge(x2T_ready, c)
                for j in range(CT):
                    m = pe.transpose(x2T_ps[:, P * j:P * (j + 1)], xn[:, j, :], ident[:, :])
                m.then_inc(x2T_filled, 1)

            def gate_up(c, par):
                pe.wait_ge(x2T_ready, c + 1)
                hi = x2T_hi[:, ds(par, 1), :].rearrange("p a n -> p (a n)")
                lo = x2T_lo[:, ds(par, 1), :].rearrange("p a n -> p (a n)")
                for j in range(HB):
                    if not (isinstance(c, int) and c == 0):
                        pe.wait_ge(hidden_ready, HB * (c - 1) + j + 1)
                    for o, w in ((gate_ps[j], j), (up_ps[j], HB + j)):
                        pe.matmul(o, wguT[:, 0, w, :], hi, start=True, stop=False)
                        pe.matmul(o, wguT[:, 0, w, :], lo, start=False, stop=False)
                        m = pe.matmul(o, wguT[:, 1, w, :], hi, start=False, stop=True)
                    m.then_inc(gate_up_ready, 1)

            def down(c):
                pe.wait_ge(hidden_ready, HB * (c + 1))
                pe.wait_ge(result_ready, c)
                for j in range(CT):
                    for k in range(HB):
                        m = pe.matmul(down_ps[:, P * j:P * (j + 1)], hidden[:, k, P * j:P * (j + 1)], wdT[:, k, :],
                                      start=(k == 0), stop=(k == HB - 1))
                m.then_inc(down_ready, 1)

            transpose_x2(0)
            transpose_x2(1)
            gate_up(0, 0)
            with pe.Fori(1, NCH - 1) as c:
                transpose_x2(c + 1)
                gate_up(c, pe.snap(c % 2))
                down(c - 1)
            gate_up(NCH - 1, (NCH - 1) % 2)
            down(NCH - 2)
            down(NCH - 1)

        @block.vector
        def _(dve):
            step = [0]
            def link(ins):
                step[0] += 1
                ins.then_inc(w_step, 1)
                dve.wait_ge(w_step, step[0])

            def statistics(n, ntiles, tile):
                if not (isinstance(n, int) and n == 0):
                    dve.wait_ge(xn_ready, HALVES * n if ntiles == TB else HALVES * B + n - B)
                for j in range(ntiles):
                    m = dve.bn_stats(stats[:, j, :], tile(j))
                m.then_inc(stats_done, 1)

            def attention_stats(b):
                statistics(b, TB, lambda j: xs[:, ds(TB * b + j, 1), :].rearrange("p a n -> p (a n)"))

            def ffn_stats(c):
                statistics(B + c, CT, lambda j: xs[:, ds(CT * c + j, 1), :].rearrange("p a n -> p (a n)"))

            def weights():
                dve.wait_ge(w_loaded, 96)
                link(dve.tensor_copy(wgu_in[:, :, :], wgu_int[:, :, :]))
                link(dve.tensor_copy(wd_in[:, :], wd_int[:, :]))
                for n, w in enumerate((wqk_in[:, :], wv_in[:, :], wgu_in[:, :, :].rearrange("p a n -> p (a n)"), wd_in[:, :])):
                    m = dve.tensor_reduce(wmax[:, n:n + 1], w, AX_X, ALU.max, apply_absolute_value=True)
                m.then_inc(w_max_ready, 1)
                dve.wait_ge(w_pe, 1)
                link(dve.tensor_reduce(wmax_row[:, :], attn_ps[0:4, 0:P], AX_X, ALU.max))
                link(dve.tensor_scalar(wmax_row[:, :], wmax_row[:, :], 1.0e-30, None, ALU.max))
                link(dve.tensor_scalar(wpow_row[:, :].bitcast(U32), wmax_row[:, :].bitcast(U32), EXPONENT_BITS, None,
                                       ALU.bitwise_and))
                link(dve.tensor_scalar(wpow_diag[:, :], ident[0:4, 0:4], wpow_row[:, 0:1], None, ALU.mult))
                assert step[0] == W_DIAG
                dve.wait_ge(w_pe, 3)
                link(dve.tensor_copy(wpow[:, :], attn_ps[:, 256:260]))
                link(dve.reciprocal(wpow_inv[:, :], wpow[:, :]))
                link(dve.tensor_scalar(score_scale[:, :], wpow[:, 0:1], SCALE, None, ALU.mult))
                link(dve.tensor_scalar(neg_score_scale[:, :], score_scale[:, :], -1.0, None, ALU.mult))
                link(dve.reciprocal(score_inv[:, :], score_scale[:, :]))
                link(dve.tensor_tensor(slope_scaled[:, :], slope_col[:, :], score_inv[:, :], ALU.mult))
                dve.wait_ge(distance_ready, 1)
                dve.tensor_scalar(bias_raw[:, :], distance[:, :], slope_scaled[:, 0:1], None, ALU.mult)\
                   .then_inc(bias_raw_ready, 1)
                dve.tensor_scalar(wtmp[:, 0, :], wqk_in[:, :], wpow_inv[:, 0:1], None, ALU.mult)
                link(dve.tensor_scalar(wtmp[:, 1, :], work_ps[:, 0, 0:P], wpow_inv[:, 1:2], None, ALU.mult))
                dve.tensor_copy(wqk[:, 0, :], wtmp[:, 0, :])
                link(dve.tensor_copy(wvT[:, 0, :], wtmp[:, 1, :]))
                dve.tensor_tensor(wqk[:, 1, :], wtmp[:, 0, :], wqk[:, 0, :], ALU.subtract)
                link(dve.tensor_tensor(wvT[:, 1, :], wtmp[:, 1, :], wvT[:, 0, :], ALU.subtract))
                dve.tensor_copy(wdT[:, :, :].rearrange("p a n -> p (a n)"), work_ps[:, 0, P:P * (HB + 1)])\
                   .then_inc(w_ready, 1)

            def ffn_weights():
                link(dve.tensor_scalar(gu_scale[:, :], wpow_inv[:, 2:3], F16_EXACT, 1.0, ALU.mult, ALU.min))
                link(dve.reciprocal(gu_unscale[:, :], gu_scale[:, :]))
                dve.tensor_scalar(gate_scale[:, :], gu_unscale[:, :], DEQUANT, None, ALU.mult)
                link(dve.tensor_scalar(ffn_scale[:, :], gu_unscale[:, :], DEQUANT * DEQUANT, None, ALU.mult))
                for g in range(2):
                    m = dve.tensor_scalar(wguT_f[:, HB * g:HB * (g + 1), :].rearrange("p a n -> p (a n)"),
                                          score_ps[:, g, 0:HB * P], gu_scale[:, 0:1], None, ALU.mult)
                link(m)
                link(dve.tensor_copy(wguT[:, 0, :, :], wguT_f[:, :, :]))
                dve.tensor_tensor(wguT[:, 1, :, :], wguT_f[:, :, :], wguT[:, 0, :, :], ALU.subtract).then_inc(w_ready, 1)

            def split_low(b, par, kind, h):
                bank, used = bank_use(b, (kind, h), True)
                hi, lo = (xT_hi, xT_lo) if kind == "xT" else (qT_hi, qT_lo)
                dve.wait_ge(hi_ready, 2 * HALVES * b + (HALVES if kind == "q" else 0) + h + 1)
                cols = slice(CW * h, CW * h + CW)
                dve.tensor_tensor(lo[:, ds(par, 1), cols].rearrange("p a n -> p (a n)"), work_ps[:, bank, :],
                                  hi[:, ds(par, 1), cols].rearrange("p a n -> p (a n)"), ALU.subtract)\
                   .then_inc(work_emptied[bank], 1)

            def inverse_sum(b, i):
                dve.wait_ge(probs_ready, TB * b + i + 1)
                dve.reciprocal(inv_sum[:, i:i + 1], prob_sum[:, i:i + 1]).then_inc(inv_ready, 1)

            def bias_scores(i):
                n = P * (i + 1)
                dve.tensor_tensor_reduce(biased[:, i % 2, 0:n], score_ps[:, i % 2, 0:n], bias[:, S - n:S],
                                         neg_score_scale[:, 0:1], 3.0e38, ALU.add, ALU.min, neg_max[:, i:i + 1])\
                   .then_inc(biased_ready, 1)

            def add_attention(b, i):
                t = TB * b + i
                dve.wait_ge(inv_ready, t + 1)
                dve.wait_ge(attn_ready, t + 1)
                row = xs[:, ds(t, 1), :].rearrange("p a n -> p (a n)")
                dve.scalar_tensor_tensor(row, attn_ps[:, 0:D], inv_sum[:, i:i + 1], row, ALU.mult, ALU.add)\
                   .then_inc(attn_added, 1)

            def batch(b, par, nxt, final):
                for i in range(TB):
                    if i == 0 and not final:
                        if isinstance(b, int):
                            dve.wait_ge(x_loaded[b + 1], 16)
                        attention_stats(b + 1)
                    if i + 2 < TB or not final:
                        dve.wait_ge(scores_ready, TB * b + i + 3)
                    inverse_sum(b, i)
                    if i + 2 < TB or not final:
                        bias_scores((i + 2) % TB)
                    if not final and 1 <= i <= 4:
                        split_low(b + 1, nxt, *prologue[i - 1])
                    add_attention(b, i)

            dve.wait_ge(x_loaded[0], 16)
            attention_stats(0)
            weights()
            for part in prologue[:4]:
                split_low(0, 0, *part)
            ffn_weights()
            dve.wait_ge(bias_ready, 1)
            for i in range(2):
                dve.wait_ge(scores_ready, i + 1)
                bias_scores(i)
            for b in range(1, B):
                dve.wait_ge(x_loaded[b], 16)
            with dve.Fori(0, B - 1) as b:
                batch(b, dve.snap(b % 2), dve.snap((b + 1) % 2), False)
            batch(B - 1, (B - 1) % 2, B % 2, True)

            def split_x2(c, par):
                dve.wait_ge(x2T_hi_ready, c + 1)
                dve.tensor_tensor(x2T_lo[:, ds(par, 1), :].rearrange("p a n -> p (a n)"), x2T_ps,
                                  x2T_hi[:, ds(par, 1), :].rearrange("p a n -> p (a n)"), ALU.subtract)\
                   .then_inc(x2T_ready, 1)

            def multiply(c):
                if not (isinstance(c, int) and c == 0):
                    dve.wait_ge(down_ready, c)
                for j in range(HB):
                    dve.wait_ge(silu_ready, HB * c + j + 1)
                    dve.tensor_tensor(hidden[:, j, :], up_ps[j], silu[:, j, :], ALU.mult).then_inc(hidden_ready, 1)

            def add_ffn(c):
                dve.wait_ge(down_ready, c + 1)
                rows = xs[:, ds(CT * c, CT), :].rearrange("p a n -> p (a n)")
                dve.scalar_tensor_tensor(rows, down_ps, ffn_scale[:, 0:1], rows, ALU.mult, ALU.add)\
                   .then_inc(result_ready, 1)

            dve.wait_ge(attn_added, NT)
            ffn_stats(0)
            split_x2(0, 0)
            ffn_stats(1)
            split_x2(1, 1)
            multiply(0)
            with dve.Fori(1, NCH - 1) as c:
                ffn_stats(c + 1)
                split_x2(c + 1, dve.snap((c + 1) % 2))
                add_ffn(c - 1)
                multiply(c)
            add_ffn(NCH - 2)
            multiply(NCH - 1)
            add_ffn(NCH - 1)

        @block.scalar
        def _(act):
            def copy_high(b, par, kind, h):
                bank, used = bank_use(b, (kind, h), True)
                hi = xT_hi if kind == "xT" else qT_hi
                act.wait_ge(work_filled[bank], used + 1)
                act.copy(hi[:, ds(par, 1), CW * h:CW * h + CW].rearrange("p a n -> p (a n)"), work_ps[:, bank, :])\
                   .then_inc(hi_ready, 1)

            def copy_v(b, par, h):
                bank, used = bank_use(b, ("v", h), True)
                act.wait_ge(work_filled[bank], used + 1)
                act.activation(v[:, ds(par, 1), CW * h:CW * h + CW].rearrange("p a n -> p (a n)"), work_ps[:, bank, :],
                               ACT.Copy, scale=wpow[:, 1:2]).then_inc(work_emptied[bank], 1)

            def prologue_part(b, par, kind, h):
                if kind == "v":
                    copy_v(b, par, h)
                else:
                    copy_high(b, par, kind, h)

            def exponentials(b, i):
                act.wait_ge(biased_ready, TB * b + i + 1)
                n = P * (i + 1)
                act.activation(probs[:, i % 2, 0:n], biased[:, i % 2, 0:n], ACT.Exp, bias=neg_max[:, i:i + 1],
                               scale=-1.0, accum_out=prob_sum[:, i:i + 1]).then_inc(probs_ready, 1)

            def copy_probsT(b, i):
                for h in range(i // CT + 1):
                    bank, used = bank_use(b, (i, h), False)
                    n = P * min(CT, i + 1 - CT * h)
                    act.wait_ge(work_filled[bank], used + 1)
                    act.copy(probsT[:, i % 2, CW * h:CW * h + n], work_ps[:, bank, 0:n]).then_inc(work_emptied[bank], 1)

            def batch(b, par, nxt, final):
                for i in range(TB):
                    copy_probsT(b, i)
                    if not final and 1 <= i <= PRO:
                        prologue_part(b + 1, nxt, *prologue[i - 1])
                    if i + 2 < TB:
                        exponentials(b, i + 2)
                    elif not final:
                        exponentials(b + 1, i + 2 - TB)

            act.wait_ge(w_ready, 1)
            for part in prologue:
                prologue_part(0, 0, *part)
            exponentials(0, 0)
            exponentials(0, 1)
            with act.Fori(0, B - 1) as b:
                batch(b, act.snap(b % 2), act.snap((b + 1) % 2), False)
            batch(B - 1, (B - 1) % 2, B % 2, True)

            def copy_x2_high(c, par):
                act.wait_ge(x2T_filled, c + 1)
                act.copy(x2T_hi[:, ds(par, 1), :].rearrange("p a n -> p (a n)"), x2T_ps).then_inc(x2T_hi_ready, 1)

            def silus(c):
                for j in range(HB):
                    act.wait_ge(gate_up_ready, HB * c + j + 1)
                    act.activation(silu[:, j, :], gate_ps[j], ACT.Silu, scale=gate_scale[:, 0:1]).then_inc(silu_ready, 1)

            copy_x2_high(0, 0)
            copy_x2_high(1, 1)
            silus(0)
            with act.Fori(1, NCH - 1) as c:
                copy_x2_high(c + 1, act.snap((c + 1) % 2))
                silus(c)
            silus(NCH - 1)


_INS = ['L0_attn_x', 'L0_attn_W_qk', 'L0_attn_W_v', 'L0_attn_alibi_slope', 'L0_ffn_w_gate', 'L0_ffn_w_up', 'L0_ffn_w_down']


def kernel(**inputs):
    import numpy as _np
    import concourse.bacc as _bacc
    from concourse import mybir as _mybir
    from concourse.bass_utils import run_bass_kernel_spmd as _run

    nc = _bacc.Bacc("TRN2", target_bir_lowering=False, num_devices=1)
    arrays, args = {}, []
    for name in _INS:
        a = _np.ascontiguousarray(inputs[name])
        arrays[f"in_{name}_dram"] = a
        args.append(nc.dram_tensor(f"in_{name}_dram", a.shape, _mybir.dt.from_np(a.dtype), kind="ExternalInput").ap())
    shape = inputs['L0_attn_x'].shape
    args.append(nc.dram_tensor("out_0_dram", shape, _mybir.dt.float32, kind="ExternalOutput").ap())
    preln_block(nc, *args)
    r = _run(nc, [arrays], core_ids=[0])
    return r.results[0]["out_0_dram"]
```

```python
from contextlib import ExitStack

import concourse.bass as bass
from concourse import mybir

ALU = mybir.AluOpType
ACT = mybir.ActivationFunctionType
F32 = mybir.dt.float32
F16 = mybir.dt.float16
I32 = mybir.dt.int32
U32 = mybir.dt.uint32
AX_X = mybir.AxisListType.X
ds = bass.ds

P = 128
EPS = 1e-5
DEQUANT = 1.0 / 127.0
EXPONENT_BITS = 0x7F800000
F16_EXACT = 1024.0
HIDDEN_UNIT = 32.0
MASKED = -3.0e38


def preln_block(nc, x, w_qk, w_v, slope, w_gate, w_up, w_down, out):
    B, S, D = x.shape
    HID = w_gate.shape[0]
    TB = S // P
    NT = B * TB
    HB = HID // P
    CT = 4
    CW = CT * P
    NCH = NT // CT
    HALVES = S // CW
    SCALE = float(D) ** -0.5
    assert D == P and S == 2 * CW and HID % P == 0

    NWORK = 3
    prologue = [(kind, h) for kind in ("xT", "q", "v") for h in range(HALVES)]
    probs_groups = [[(i, h) for h in range(i // CT + 1)] for i in range(TB)]
    opening = prologue + [(0, 0)]
    middle, closing = [], []
    for i in range(TB):
        middle += probs_groups[(i + 1) % TB] + prologue[i:i + 1]
        if i + 1 < TB:
            closing += probs_groups[i + 1]
        closing += prologue[:HALVES][i:i + 1]
    assert len(middle) % NWORK == 0

    def place(around, group):
        if isinstance(around, int) and around < 0:
            n = opening.index(group)
            return n % NWORK, n
        n = len(opening) + (closing if isinstance(around, int) and around == B - 1 else middle).index(group)
        return n % NWORK, around * len(middle) + n

    def probs_place(b, i, h):
        return place(b if i else b - 1, (i, h))

    WORK_USES = len(opening) + (B - 1) * len(middle) + len(closing)
    assert middle[-1] == opening[-1] == (0, 0)

    def at(buffer, half, columns):
        if isinstance(half, int):
            return buffer[:, half, columns]
        return buffer[:, ds(half, 1), columns].rearrange("p a n -> p (a n)")

    with ExitStack() as ctx:
        def sb(name, shape, dt):
            return ctx.enter_context(nc.sbuf_tensor(name, shape, dt))

        def sem(name):
            return ctx.enter_context(nc.semaphore(name))

        wqk_in = sb("wqk_in", [P, D], F32)
        wv_in = sb("wv_in", [P, D], F32)
        wgu_int = sb("wgu_int", [P, 2 * HB, D], I32)
        wd_int = sb("wd_int", [P, HID], I32)
        wgu_in = sb("wgu_in", [P, 2 * HB, D], F32)
        wd_in = sb("wd_in", [P, HID], F32)
        slope_col = sb("slope_col", [P, 1], F32)
        ident = sb("ident", [P, P], F32)
        ones2 = sb("ones2", [2, P], F32)
        warm = sb("warm", [P, 1], F32)
        wmax = sb("wmax", [P, 4], F32)
        wmax_row = sb("wmax_row", [2, 2], F32)
        wpow_row = sb("wpow_row", [2, 2], F32)
        wpow_diag = sb("wpow_diag", [2, 2, 2], F32)
        wpow = sb("wpow", [P, 4], F32)
        wpow_inv = sb("wpow_inv", [P, 4], F32)
        int_scale = sb("int_scale", [P, 2], F32)
        int_unscale = sb("int_unscale", [P, 2], F32)
        min_int_scale = sb("min_int_scale", [1, 1], F32)
        gu_square = sb("gu_square", [P, 1], F32)
        gu_inv_square = sb("gu_inv_square", [P, 1], F32)
        hidden_scale = sb("hidden_scale", [P, 1], F32)
        gate_scale = sb("gate_scale", [P, 1], F32)
        ffn_scale = sb("ffn_scale", [P, 1], F32)
        score_scale = sb("score_scale", [P, 1], F32)
        neg_score_scale = sb("neg_score_scale", [P, 1], F32)
        score_inv = sb("score_inv", [P, 1], F32)
        slope_scaled = sb("slope_scaled", [P, 1], F32)
        distance = sb("distance", [P, S], F32)
        bias_raw = sb("bias_raw", [P, S], F32)
        bias = sb("bias", [P, S], F32)
        wtmp = sb("wtmp", [P, 2, D], F32)
        wqk = sb("wqk", [P, 2, D], F16)
        wvT = sb("wvT", [P, 2, D], F16)
        wguT_f = sb("wguT_f", [P, 2 * HB, P], F32)
        wguT = sb("wguT", [P, 2, 2 * HB, P], F16)
        wdT_f = sb("wdT_f", [P, HB * D], F32)
        wdT = sb("wdT", [P, 2, HB, D], F16)
        split_flag = sb("split_flag", [1, 1], I32)
        norm_const = sb("norm_const", [P, 5], F32)

        xs = sb("xs", [P, NT, D], F32)
        stats = sb("stats", [P, TB, 6], F32)
        mean_sum = sb("mean_sum", [P, TB], F32)
        mean_dif = sb("mean_dif", [P, TB], F32)
        dif_sq = sb("dif_sq", [P, TB], F32)
        square_sum = sb("square_sum", [P, TB], F32)
        between = sb("between", [P, TB], F32)
        within = sb("within", [P, TB], F32)
        within_eps = sb("within_eps", [P, TB], F32)
        mean = sb("mean", [P, TB], F32)
        var_eps = sb("var_eps", [P, TB], F32)
        rstd = sb("rstd", [P, TB], F32)
        centred = sb("centred", [P, TB, D], F32)
        xn = sb("xn", [P, TB, D], F32)
        xT_hi = sb("xT_hi", [P, 2, S], F16)
        xT_lo = sb("xT_lo", [P, 2, S], F16)
        qT_hi = sb("qT_hi", [P, 2, S], F16)
        qT_lo = sb("qT_lo", [P, 2, S], F16)
        v_hi = sb("v_hi", [P, 2, S], F16)
        v_lo = sb("v_lo", [P, 2, S], F16)
        biased = sb("biased", [P, 2, S], F32)
        probs = sb("probs", [P, 2, S], F32)
        probsT_hi = sb("probsT_hi", [P, 2, S], F16)
        probsT_lo = sb("probsT_lo", [P, 2, S], F16)
        neg_max = sb("neg_max", [P, TB], F32)
        prob_sum = sb("prob_sum", [P, TB], F32)
        scaled_sum = sb("scaled_sum", [P, TB], F32)
        inv_sum = sb("inv_sum", [P, TB], F32)
        silu = sb("silu", [P, 2, HB, CW], F32)
        hidden = sb("hidden", [P, 2, HB, CW], F32)
        x2T_hi, x2T_lo = (part[:, B % 2, :].rearrange("p (c n) -> p c n", c=2) for part in (xT_hi, xT_lo))
        hidden_hi = sb("hidden_hi", [P, 2, HB, CW], F16)
        hidden_lo = sb("hidden_lo", [P, 2, HB, CW], F16)

        score_ps = ctx.enter_context(nc.psum_tensor("score_ps", [P, 2, S], F32))
        attn_ps = ctx.enter_context(nc.psum_tensor("attn_ps", [P, 512], F32))
        work_ps = ctx.enter_context(nc.psum_tensor("work_ps", [P, NWORK, 512], F32))
        gate_ps = [score_ps[:, 0, 0:CW], score_ps[:, 1, 0:CW], work_ps[:, 0, :]]
        up_ps = [score_ps[:, 0, CW:S], score_ps[:, 1, CW:S], work_ps[:, 1, :]]
        x2T_ps = work_ps[:, 2, :]
        gate_up_w_ps = [score_ps[:, 0, 0:HID], score_ps[:, 0, CW:CW + HID]]
        down_w_ps = score_ps[:, 1, 0:HID]
        v_w_ps = score_ps[:, 1, CW:CW + D]
        down_ps = attn_ps[:, :]

        x_loaded = [sem(f"x_loaded{b}") for b in range(B)]
        attn_w_loaded = sem("attn_w_loaded")
        ffn_w_loaded = sem("ffn_w_loaded")
        const_ready = sem("const_ready")
        ident_ready = sem("ident_ready")
        w_step = sem("w_step")
        w_max_ready = sem("w_max_ready")
        w_max_turned = sem("w_max_turned")
        w_diag_ready = sem("w_diag_ready")
        w_pow_spread = sem("w_pow_spread")
        w_pow_copied = sem("w_pow_copied")
        wv_turned = sem("wv_turned")
        ffn_w_float = sem("ffn_w_float")
        ffn_w_turned = sem("ffn_w_turned")
        ffn_w_copied = sem("ffn_w_copied")
        attn_w_ready = sem("attn_w_ready")
        ffn_w_hi_ready = sem("ffn_w_hi_ready")
        split_flag_ready = sem("split_flag_ready")
        ffn_w_ready = sem("ffn_w_ready")
        distance_ready = sem("distance_ready")
        bias_raw_ready = sem("bias_raw_ready")
        bias_ready = sem("bias_ready")
        stats_done = sem("stats_done")
        pool_step = sem("pool_step")
        xn_ready = sem("xn_ready")
        work_filled = sem("work_filled")
        work_emptied = sem("work_emptied")
        hi_ready = sem("hi_ready")
        probsT_hi_ready = sem("probsT_hi_ready")
        v_hi_ready = sem("v_hi_ready")
        scores_ready = sem("scores_ready")
        biased_ready = sem("biased_ready")
        probs_ready = sem("probs_ready")
        attn_ready = sem("attn_ready")
        scaled_ready = sem("scaled_ready")
        inv_ready = sem("inv_ready")
        attn_added = sem("attn_added")
        x2T_filled = sem("x2T_filled")
        x2T_hi_ready = sem("x2T_hi_ready")
        x2T_ready = sem("x2T_ready")
        gate_up_ready = sem("gate_up_ready")
        silu_ready = sem("silu_ready")
        hidden_ready = sem("hidden_ready")
        hidden_hi_ready = sem("hidden_hi_ready")
        hidden_lo_ready = sem("hidden_lo_ready")
        last_lo_ready = sem("last_lo_ready")
        down_ready = sem("down_ready")
        result_ready = sem("result_ready")
        stored = sem("stored")

        N_READ, N_SMALL = 3, 10
        N_STEPS = N_SMALL + HALVES

        block = ctx.enter_context(nc.Block())

        @block.sync
        def _(sp):
            xv = x.rearrange("b (j p) d -> b p j d", p=P)
            ov = out.rearrange("b (j p) d -> p (b j) d", p=P)
            sp.dma_start(xs[:, 0:TB, :], xv[0]).then_inc(x_loaded[0], 16)
            sp.dma_start(wqk_in[:, :], w_qk).then_inc(attn_w_loaded, 16)
            sp.dma_start(wv_in[:, :], w_v).then_inc(attn_w_loaded, 16)
            sp.dma_start(slope_col[:, :], slope.rearrange("(a d) -> a d", a=1).broadcast_to([P, 1])).then_inc(attn_w_loaded, 16)
            sp.dma_start(xs[:, TB:2 * TB, :], xv[1]).then_inc(x_loaded[1], 16)
            sp.dma_start(wgu_int[:, 0:HB, :], w_gate.rearrange("(j p) d -> p j d", p=P)).then_inc(ffn_w_loaded, 16)
            sp.dma_start(wgu_int[:, HB:2 * HB, :], w_up.rearrange("(j p) d -> p j d", p=P)).then_inc(ffn_w_loaded, 16)
            sp.dma_start(wd_int[:, :], w_down).then_inc(ffn_w_loaded, 16)
            for b in range(2, B):
                sp.dma_start(xs[:, TB * b:TB * (b + 1), :], xv[b]).then_inc(x_loaded[b], 16)
            with sp.Fori(0, NCH) as c:
                sp.wait_ge(result_ready, c + 1)
                sp.dma_start(ov[:, ds(CT * c, CT), :], xs[:, ds(CT * c, CT), :]).then_inc(stored, 16)
            sp.wait_ge(stored, 16 * NCH)

        @block.gpsimd
        def _(pool):
            pool.memset(ident[:, :], 0.0).then_inc(const_ready, 1)
            pool.memset(ones2[:, :], 1.0).then_inc(const_ready, 1)
            for n, value in enumerate((0.5, 0.25, 1.0 / D, EPS, -0.5)):
                pool.memset(norm_const[:, n:n + 1], value).then_inc(const_ready, 1)
            pool.wait_ge(const_ready, 7)
            pool.affine_select(out=ident[:, :], in_=ident[:, :], compare_op=ALU.not_equal, fill=1.0, base=0,
                               pattern=[[-1, P]], channel_multiplier=1).then_inc(ident_ready, 1)
            pool.iota(distance[:, :], pattern=[[1, S]], base=P - S, channel_multiplier=-1,
                      allow_small_or_imprecise_dtypes=True).then_inc(distance_ready, 1)

            def tiles_of(n, h):
                return xs[:, ds(TB * (n % B) + CT * h, CT), :]

            def per_row(column, t):
                return column[:, t].rearrange("p (t a) -> p t a", a=1).broadcast_to([P, CT, D])

            def moments(n):
                steps = N_STEPS * n
                half, quarter, per_element, eps, power = (norm_const[:, k:k + 1].broadcast_to([P, TB]) for k in range(5))

                def small(out, a, b, op):
                    pool.tensor_tensor(out[:, :], a, b, op).then_inc(pool_step, 1)

                pool.wait_ge(stats_done, n + 1)
                small(mean_sum, stats[:, :, 1], stats[:, :, 4], ALU.add)
                small(mean_dif, stats[:, :, 1], stats[:, :, 4], ALU.subtract)
                small(square_sum, stats[:, :, 2], stats[:, :, 5], ALU.add)
                pool.wait_ge(pool_step, steps + N_READ)
                small(mean, mean_sum[:, :], half, ALU.mult)
                small(dif_sq, mean_dif[:, :], mean_dif[:, :], ALU.mult)
                small(within, square_sum[:, :], per_element, ALU.mult)
                pool.wait_ge(pool_step, steps + 6)
                small(between, dif_sq[:, :], quarter, ALU.mult)
                small(within_eps, within[:, :], eps, ALU.add)
                pool.wait_ge(pool_step, steps + 8)
                small(var_eps, within_eps[:, :], between[:, :], ALU.add)
                pool.wait_ge(pool_step, steps + 9)
                small(rstd, var_eps[:, :], power, ALU.pow)

            def centre(n):
                pool.wait_ge(pool_step, N_STEPS * n + 4)
                for h in range(HALVES):
                    t = slice(CT * h, CT * h + CT)
                    pool.tensor_tensor(centred[:, t, :], tiles_of(n, h), per_row(mean, t), ALU.subtract)\
                        .then_inc(pool_step, 1)

            def scale(n):
                if isinstance(n, int) and n > B + 1:
                    pool.wait_ge(x2T_filled, HALVES * (n - B - 1))
                elif not (isinstance(n, int) and n == 0):
                    pool.wait_ge(work_filled, place(n - 2, ("xT", HALVES - 1))[1] + 1)
                for h in range(HALVES):
                    t = slice(CT * h, CT * h + CT)
                    pool.wait_ge(pool_step, N_STEPS * n + N_SMALL + h + 1)
                    pool.tensor_tensor(xn[:, t, :], centred[:, t, :], per_row(rstd, t), ALU.mult).then_inc(xn_ready, 1)

            def norm(n):
                moments(n)
                centre(n)
                scale(n)

            def hidden_low(c, par):
                for j in range(HB - 1):
                    pool.wait_ge(hidden_hi_ready, HB * c + j + 1)
                    pool.tensor_tensor(hidden_lo[:, par, j, :], hidden[:, par, j, :], hidden_hi[:, par, j, :],
                                       ALU.subtract).then_inc(hidden_lo_ready, 1)

            norm(0)
            moments(1)
            centre(1)
            pool.wait_ge(bias_raw_ready, 1)
            pool.affine_select(out=bias[:, :], in_=bias_raw[:, :], compare_op=ALU.is_ge, fill=MASKED,
                               base=S - P, pattern=[[-1, S]], channel_multiplier=1).then_inc(bias_ready, 1)
            scale(1)
            pool.wait_ge(ffn_w_hi_ready, 1)
            pool.tensor_tensor(wguT[:, 1, :, :], wguT_f[:, :, :], wguT[:, 0, :, :], ALU.subtract).then_inc(ffn_w_ready, 1)
            pool.tensor_tensor(wdT[:, 1, :, :].rearrange("p a n -> p (a n)"), wdT_f[:, :],
                               wdT[:, 0, :, :].rearrange("p a n -> p (a n)"), ALU.subtract).then_inc(ffn_w_ready, 1)
            with pool.Fori(2, B + 1) as n:
                norm(n)
            norm(B + 1)
            moments(B + 2)
            centre(B + 2)
            hidden_low(0, 0)
            scale(B + 2)
            moments(B + 3)
            hidden_low(1, 1)
            centre(B + 3)
            hidden_low(2, 0)
            hidden_low(3, 1)
            scale(B + 3)
            with pool.Fori(2, NCH // 2) as m:
                for par in range(2):
                    hidden_low(2 * m + par, par)

        @block.tensor
        def _(pe):
            def spread_powers(pair):
                pe.wait_ge(w_max_ready, pair + 1)
                pe.transpose(attn_ps[0:2, 0:P], wmax[:, 2 * pair:2 * pair + 2], ident[:, :]).then_inc(w_max_turned, 1)
                pe.wait_ge(w_diag_ready, pair + 1)
                pe.matmul(attn_ps[:, 256:258], ones2[:, :], wpow_diag[:, pair, :], start=True, stop=True)\
                  .then_inc(w_pow_spread, 1)

            def fill(bank, number, emit):
                if not (isinstance(number, int) and number < NWORK):
                    pe.wait_ge(work_emptied, number - NWORK + 1)
                emit(work_ps[:, bank, :]).then_inc(work_filled, 1)

            def taken(bank, number):
                pe.wait_ge(work_emptied, number + 1)

            def three(o, left, right):
                (l_hi, l_lo), (r_hi, r_lo) = left, right
                pe.matmul(o, l_hi, r_hi, start=True, stop=False)
                pe.matmul(o, l_hi, r_lo, start=False, stop=False)
                return pe.matmul(o, l_lo, r_hi, start=False, stop=True)

            def prologue_part(b, par, kind, h):
                cols = slice(CW * h, CW * h + CW)

                def transpose_x(ps):
                    for j in range(CT):
                        m = pe.transpose(ps[:, P * j:P * (j + 1)], xn[:, CT * h + j, :], ident[:, :])
                    return m

                def project_q(ps):
                    return three(ps, (wqk[:, 0, :], wqk[:, 1, :]), (at(xT_hi, par, cols), at(xT_lo, par, cols)))

                def project_v(ps):
                    for j in range(CT):
                        tok = slice(CW * h + P * j, CW * h + P * j + P)
                        m = three(ps[:, P * j:P * j + P], (at(xT_hi, par, tok), at(xT_lo, par, tok)),
                                  (wvT[:, 0, :], wvT[:, 1, :]))
                    return m

                if kind == "xT":
                    pe.wait_ge(xn_ready, HALVES * b + h + 1)
                else:
                    taken(*place(b - 1, ("xT", h)))
                fill(*place(b - 1, (kind, h)), {"xT": transpose_x, "q": project_q, "v": project_v}[kind])

            def scores(b, par, i):
                t = TB * b + i
                if i < 3:
                    taken(*place(b - 1, ("q", 0)))
                if not (isinstance(t, int) and t < 2):
                    pe.wait_ge(biased_ready, t - 1)
                rows = slice(P * i, P * (i + 1))
                for k0 in range(0, P * (i + 1), CW):
                    keys = slice(k0, min(k0 + CW, P * (i + 1)))
                    m = three(score_ps[:, i % 2, keys], (at(qT_hi, par, rows), at(qT_lo, par, rows)),
                              (at(xT_hi, par, keys), at(xT_lo, par, keys)))
                m.then_inc(scores_ready, 1)

            def transpose_probs(b, i):
                pe.wait_ge(probs_ready, TB * b + i + 1)
                for h in range(i // CT + 1):
                    def emit(ps, h=h):
                        for j in range(min(CT, i + 1 - CT * h)):
                            k0 = CW * h + P * j
                            m = pe.transpose(ps[:, P * j:P * (j + 1)], probs[:, i % 2, k0:k0 + P], ident[:, :])
                        return m
                    fill(*probs_place(b, i, h), emit)

            def weigh_values(b, par, i):
                if i == 0:
                    pe.wait_ge(work_emptied, len(opening) + len(middle) * b)
                else:
                    taken(*probs_place(b, i, i // CT))
                pe.wait_ge(attn_added, TB * b + i)
                for j in range(i + 1):
                    keys = slice(P * j, P * (j + 1))
                    p_hi, p_lo = probsT_hi[:, i % 2, keys], probsT_lo[:, i % 2, keys]
                    v_j = at(v_hi, par, keys)
                    pe.matmul(attn_ps[:, 0:D], p_hi, v_j, start=(j == 0), stop=False)
                    pe.matmul(attn_ps[:, 0:D], p_hi, at(v_lo, par, keys), start=False, stop=False)
                    m = pe.matmul(attn_ps[:, 0:D], p_lo, v_j, start=False, stop=(j == i))
                m.then_inc(attn_ready, 1)

            def around(b, par, nxt, final):
                for i in range(TB):
                    if i + 3 < TB:
                        scores(b, par, i + 3)
                    elif not final:
                        scores(b + 1, nxt, i + 3 - TB)
                    if i + 1 < TB:
                        transpose_probs(b, i + 1)
                    elif not final:
                        transpose_probs(b + 1, 0)
                    if i < (HALVES if final else len(prologue)):
                        prologue_part(b + 1, nxt, *prologue[i])
                    weigh_values(b, par, i)

            pe.wait_ge(ident_ready, 1)
            pe.wait_ge(attn_w_loaded, 48)
            pe.transpose(v_w_ps, wv_in[:, :], ident[:, :]).then_inc(wv_turned, 1)
            spread_powers(0)
            for part in prologue[:2]:
                prologue_part(0, 0, *part)
            pe.wait_ge(ffn_w_float, 2)
            for j in range(2 * HB):
                pe.transpose(gate_up_w_ps[j // HB][:, P * (j % HB):P * (j % HB + 1)], wgu_in[:, j, :], ident[:, :])
            for j in range(HB):
                m = pe.transpose(down_w_ps[:, P * j:P * (j + 1)], wd_in[:, P * j:P * (j + 1)], ident[:, :])
            m.then_inc(ffn_w_turned, 1)
            pe.wait_ge(attn_w_ready, 1)
            for part in prologue[2:4]:
                prologue_part(0, 0, *part)
            spread_powers(1)
            pe.wait_ge(ffn_w_copied, 3)
            scores(0, 0, 0)
            scores(0, 0, 1)
            for part in prologue[4:]:
                prologue_part(0, 0, *part)
            scores(0, 0, 2)
            transpose_probs(0, 0)
            pe.wait_ge(w_pow_copied, 2)
            with pe.Fori(0, B - 1) as b:
                around(b, pe.snap(b % 2), pe.snap((b + 1) % 2), False)
            around(B - 1, (B - 1) % 2, B % 2, True)

            pe.wait_ge(biased_ready, NT)
            pe.wait_ge(work_emptied, WORK_USES)
            pe.wait_ge(ffn_w_ready, 2)
            pe.wait_ge(split_flag_ready, 1)
            needs_lo = pe.value_load(split_flag[0:1, 0:1], min_val=0, max_val=1)

            def transpose_x2(c, par):
                pe.wait_ge(xn_ready, HALVES * B + c + 1)
                if not (isinstance(c, int) and c == 2):
                    pe.wait_ge(x2T_ready, c - 2)
                for j in range(CT):
                    m = pe.transpose(x2T_ps[:, P * j:P * (j + 1)], xn[:, CT * par + j, :], ident[:, :])
                m.then_inc(x2T_filled, 1)

            def by_int_parts(product):
                with pe.If(needs_lo == 1):
                    product(True)
                with pe.Else():
                    product(False)

            def gate_up(c, par):
                if not (isinstance(c, int) and c < 2):
                    pe.wait_ge(x2T_ready, c - 1)

                def product(with_lo):
                    for j in range(HB):
                        if not (isinstance(c, int) and c == 0):
                            pe.wait_ge(hidden_ready, HB * (c - 1) + j + 1)
                        for o, w in ((gate_ps[j], j), (up_ps[j], HB + j)):
                            pe.matmul(o, wguT[:, 0, w, :], x2T_hi[:, par, :], start=True, stop=False)
                            if with_lo:
                                pe.matmul(o, wguT[:, 1, w, :], x2T_hi[:, par, :], start=False, stop=False)
                            m = pe.matmul(o, wguT[:, 0, w, :], x2T_lo[:, par, :], start=False, stop=True)
                        m.then_inc(gate_up_ready, 1)

                by_int_parts(product)

            def down(c, par):
                pe.wait_ge(hidden_lo_ready, (HB - 1) * (c + 1))
                pe.wait_ge(last_lo_ready, c + 1)
                if isinstance(c, int) and c == 0:
                    pe.wait_ge(attn_added, NT)
                else:
                    pe.wait_ge(result_ready, c)

                def product(with_lo):
                    for j in range(CT):
                        o = down_ps[:, P * j:P * (j + 1)]
                        for k in range(HB):
                            h_hi, h_lo = (h[:, par, k, P * j:P * (j + 1)] for h in (hidden_hi, hidden_lo))
                            pe.matmul(o, h_hi, wdT[:, 0, k, :], start=(k == 0), stop=False)
                            if with_lo:
                                pe.matmul(o, h_hi, wdT[:, 1, k, :], start=False, stop=False)
                            m = pe.matmul(o, h_lo, wdT[:, 0, k, :], start=False, stop=(k == HB - 1))
                    m.then_inc(down_ready, 1)

                by_int_parts(product)

            def pair(c, first, final):
                for par in range(2):
                    gate_up(c + par, par)
                    if not final:
                        transpose_x2(c + par + 2, par)
                    if not (first and par == 0):
                        down(c + par - 1, 1 - par)

            pair(0, True, False)
            with pe.Fori(1, NCH // 2 - 1) as m:
                pair(2 * m, False, False)
            pair(NCH - 2, False, True)
            down(NCH - 1, 1)

        @block.vector
        def _(dve):
            step = [0]
            def link(ins):
                step[0] += 1
                ins.then_inc(w_step, 1)
                dve.wait_ge(w_step, step[0])

            def statistics(n, j):
                if j == 0 and not (isinstance(n, int) and n == 0):
                    dve.wait_ge(pool_step, N_STEPS * (n - 1) + N_READ)
                m = dve.bn_stats(stats[:, j, :], at(xs, TB * (n % B) + j, slice(0, D)))
                if j == TB - 1:
                    m.then_inc(stats_done, 1)

            def powers_of_two(pair, least):
                cols = slice(2 * pair, 2 * pair + 2)
                dve.tensor_scalar(wmax[:, cols], wmax[:, cols], least, None, ALU.max).then_inc(w_max_ready, 1)
                dve.wait_ge(w_max_turned, pair + 1)
                link(dve.tensor_reduce(wmax_row[:, pair:pair + 1], attn_ps[0:2, 0:P], AX_X, ALU.max))
                link(dve.tensor_scalar(wpow_row[:, pair:pair + 1].bitcast(U32), wmax_row[:, pair:pair + 1].bitcast(U32),
                                       EXPONENT_BITS, None, ALU.bitwise_and))
                dve.tensor_scalar(wpow_diag[:, pair, :], ident[0:2, 0:2], wpow_row[:, pair:pair + 1], None, ALU.mult)\
                   .then_inc(w_diag_ready, 1)
                dve.wait_ge(w_pow_spread, pair + 1)
                dve.tensor_copy(wpow[:, cols], attn_ps[:, 256:258]).then_inc(w_pow_copied, 1)
                dve.wait_ge(w_pow_copied, pair + 1)
                link(dve.reciprocal(wpow_inv[:, cols], wpow[:, cols]))

            def attention_weights():
                dve.wait_ge(attn_w_loaded, 48)
                dve.tensor_reduce(wmax[:, 0:1], wqk_in[:, :], AX_X, ALU.max, apply_absolute_value=True)
                link(dve.tensor_reduce(wmax[:, 1:2], wv_in[:, :], AX_X, ALU.max, apply_absolute_value=True))
                powers_of_two(0, 1.0e-30)
                dve.wait_ge(wv_turned, 1)
                link(dve.tensor_scalar(score_scale[:, :], wpow[:, 0:1], SCALE, None, ALU.mult))
                dve.tensor_scalar(wtmp[:, 0, :], wqk_in[:, :], wpow_inv[:, 0:1], None, ALU.mult)
                link(dve.tensor_scalar(wtmp[:, 1, :], v_w_ps, wpow_inv[:, 1:2], None, ALU.mult))
                dve.reciprocal(score_inv[:, :], score_scale[:, :])
                dve.tensor_scalar(neg_score_scale[:, :], score_scale[:, :], -1.0, None, ALU.mult)
                dve.tensor_copy(wqk[:, 0, :], wtmp[:, 0, :])
                link(dve.tensor_copy(wvT[:, 0, :], wtmp[:, 1, :]))
                dve.tensor_tensor(slope_scaled[:, :], slope_col[:, :], score_inv[:, :], ALU.mult)
                dve.tensor_tensor(wqk[:, 1, :], wtmp[:, 0, :], wqk[:, 0, :], ALU.subtract)
                dve.tensor_tensor(wvT[:, 1, :], wtmp[:, 1, :], wvT[:, 0, :], ALU.subtract).then_inc(attn_w_ready, 1)
                dve.wait_ge(attn_w_ready, 1)
                dve.wait_ge(distance_ready, 1)
                dve.tensor_scalar(bias_raw[:, :], distance[:, :], slope_scaled[:, 0:1], None, ALU.mult)\
                   .then_inc(bias_raw_ready, 1)

            def ffn_maxima():
                dve.wait_ge(ffn_w_float, 2)
                dve.tensor_reduce(wmax[:, 2:3], wgu_in[:, :, :].rearrange("p a n -> p (a n)"), AX_X, ALU.max,
                                  apply_absolute_value=True)
                link(dve.tensor_reduce(wmax[:, 3:4], wd_in[:, :], AX_X, ALU.max, apply_absolute_value=True))

            def ffn_weights():
                link(dve.tensor_scalar(int_scale[:, :], wpow_inv[:, 2:4], F16_EXACT, 1.0, ALU.mult, ALU.min))
                dve.tensor_tensor(gu_square[:, :], wpow[:, 2:3], wpow[:, 2:3], ALU.mult)
                dve.tensor_tensor(gu_inv_square[:, :], wpow_inv[:, 2:3], wpow_inv[:, 2:3], ALU.mult)
                dve.tensor_reduce(min_int_scale[0:1, :], int_scale[0:1, :], AX_X, ALU.min)
                link(dve.reciprocal(int_unscale[:, :], int_scale[:, :]))
                dve.tensor_scalar(split_flag[0:1, 0:1], min_int_scale[0:1, 0:1], 1.0, None, ALU.is_lt)\
                   .then_inc(split_flag_ready, 1)
                dve.tensor_scalar(gate_scale[:, :], int_unscale[:, 0:1], DEQUANT, None, ALU.mult)
                dve.scalar_tensor_tensor(hidden_scale[:, :], gu_inv_square[:, :], HIDDEN_UNIT, int_unscale[:, 0:1],
                                         ALU.mult, ALU.mult)
                dve.scalar_tensor_tensor(ffn_scale[:, :], gu_square[:, :], DEQUANT * DEQUANT / HIDDEN_UNIT,
                                         int_unscale[:, 1:2], ALU.mult, ALU.mult)
                gu_f, gu_hi = wguT_f[:, :, :].rearrange("p a n -> p (a n)"), wguT[:, 0, :, :].rearrange("p a n -> p (a n)")
                dve.wait_ge(ffn_w_copied, 3)
                dve.tensor_scalar(gu_f, gu_f, int_scale[:, 0:1], None, ALU.mult)
                link(dve.tensor_scalar(wdT_f[:, :], wdT_f[:, :], int_scale[:, 1:2], None, ALU.mult))
                dve.tensor_copy(wdT[:, 0, :, :].rearrange("p a n -> p (a n)"), wdT_f[:, :])
                dve.tensor_copy(gu_hi, gu_f).then_inc(ffn_w_hi_ready, 1)

            def split_low(b, par, kind, h):
                bank, number = place(b - 1, (kind, h))
                hi, lo = {"xT": (xT_hi, xT_lo), "q": (qT_hi, qT_lo), "v": (v_hi, v_lo)}[kind]
                dve.wait_ge(hi_ready, len(prologue) * b + prologue.index((kind, h)) + 1)
                cols = slice(CW * h, CW * h + CW)
                dve.tensor_tensor(at(lo, par, cols), work_ps[:, bank, :], at(hi, par, cols), ALU.subtract)\
                   .then_inc(work_emptied, 1)

            def split_probsT(b, i):
                for h in range(i // CT + 1):
                    bank, number = probs_place(b, i, h)
                    n = P * min(CT, i + 1 - CT * h)
                    cols = slice(CW * h, CW * h + n)
                    dve.wait_ge(probsT_hi_ready, (TB + TB - CT) * b + i + max(0, i - CT) + h + 1)
                    dve.tensor_tensor(probsT_lo[:, i % 2, cols], work_ps[:, bank, 0:n], probsT_hi[:, i % 2, cols],
                                      ALU.subtract).then_inc(work_emptied, 1)

            def inverse_sum(b, i, more):
                t = TB * b + i
                dve.wait_ge(scaled_ready, t + 1)
                if more:
                    dve.wait_ge(probs_ready, t + 2)
                    dve.wait_ge(scores_ready, t + 4)
                dve.reciprocal(inv_sum[:, i:i + 1], scaled_sum[:, i:i + 1]).then_inc(inv_ready, 1)

            def bias_scores(i):
                n = P * (i + 1)
                dve.tensor_tensor_reduce(biased[:, i % 2, 0:n], score_ps[:, i % 2, 0:n], bias[:, S - n:S],
                                         neg_score_scale[:, 0:1], 3.0e38, ALU.add, ALU.min, neg_max[:, i:i + 1])\
                   .then_inc(biased_ready, 1)

            def add_attention(b, i):
                t = TB * b + i
                dve.wait_ge(inv_ready, t + 1)
                dve.wait_ge(attn_ready, t + 1)
                row = xs[:, ds(t, 1), :].rearrange("p a n -> p (a n)")
                dve.scalar_tensor_tensor(row, attn_ps[:, 0:D], inv_sum[:, i:i + 1], row, ALU.mult, ALU.add)\
                   .then_inc(attn_added, 1)

            def around(b, par, nxt, final):
                for i in range(TB):
                    more = i + 3 < TB or not final
                    inverse_sum(b, i, more)
                    if more:
                        bias_scores((i + 3) % TB)
                    if i + 1 < TB:
                        split_probsT(b, i + 1)
                    elif not final:
                        split_probsT(b + 1, 0)
                    if i < (HALVES if final else len(prologue)):
                        split_low(b + 1, nxt, *prologue[i])
                    if i < TB // 2:
                        statistics(b + 2, 2 * i)
                        statistics(b + 2, 2 * i + 1)
                    elif final:
                        statistics(b + 3, 2 * i - TB)
                        statistics(b + 3, 2 * i - TB + 1)
                    add_attention(b, i)

            dve.wait_ge(x_loaded[0], 16)
            for j in range(TB):
                statistics(0, j)
            attention_weights()
            dve.wait_ge(x_loaded[1], 16)
            for j in range(TB):
                statistics(1, j)
            for part in prologue[:2]:
                split_low(0, 0, *part)
            ffn_maxima()
            for part in prologue[2:4]:
                split_low(0, 0, *part)
            powers_of_two(1, 1.0)
            dve.wait_ge(bias_ready, 1)
            for i in range(2):
                dve.wait_ge(scores_ready, i + 1)
                bias_scores(i)
            for part in prologue[4:]:
                split_low(0, 0, *part)
            dve.wait_ge(scores_ready, 3)
            dve.wait_ge(probs_ready, 1)
            bias_scores(2)
            split_probsT(0, 0)
            ffn_weights()
            for b in range(2, B):
                dve.wait_ge(x_loaded[b], 16)
            with dve.Fori(0, B - 1) as b:
                around(b, dve.snap(b % 2), dve.snap((b + 1) % 2), False)
            around(B - 1, (B - 1) % 2, B % 2, True)

            def split_x2(c, par):
                dve.wait_ge(x2T_hi_ready, c - 1)
                dve.tensor_tensor(x2T_lo[:, par, :], x2T_ps, x2T_hi[:, par, :], ALU.subtract).then_inc(x2T_ready, 1)

            def multiply(c, par):
                for j in range(HB):
                    dve.wait_ge(silu_ready, HB * c + j + 1)
                    if j == 0 and not (isinstance(c, int) and c < 2):
                        dve.wait_ge(hidden_lo_ready, (HB - 1) * (c - 1))
                    dve.scalar_tensor_tensor(hidden[:, par, j, :], up_ps[j], hidden_scale[:, 0:1], silu[:, par, j, :],
                                             ALU.mult, ALU.mult).then_inc(hidden_ready, 1)

            def add_ffn(c):
                dve.wait_ge(down_ready, c + 1)
                rows = xs[:, ds(CT * c, CT), :].rearrange("p a n -> p (a n)")
                dve.scalar_tensor_tensor(rows, down_ps, ffn_scale[:, 0:1], rows, ALU.mult, ALU.add)\
                   .then_inc(result_ready, 1)

            def last_low(c, par):
                dve.wait_ge(hidden_hi_ready, HB * (c + 1))
                dve.tensor_tensor(hidden_lo[:, par, HB - 1, :], hidden[:, par, HB - 1, :],
                                  hidden_hi[:, par, HB - 1, :], ALU.subtract).then_inc(last_lo_ready, 1)

            def pair(c, first, final):
                for par in range(2):
                    multiply(c + par, par)
                    if not final:
                        split_x2(c + par + 2, par)
                    if first:
                        for j in range(TB // 2 * par, TB // 2 * (par + 1)):
                            statistics(B + 3, j)
                    if not (first and par == 0):
                        add_ffn(c + par - 1)
                    last_low(c + par, par)

            dve.wait_ge(attn_added, NT)
            pair(0, True, False)
            with dve.Fori(1, NCH // 2 - 1) as m:
                pair(2 * m, False, False)
            pair(NCH - 2, False, True)
            add_ffn(NCH - 1)

        @block.scalar
        def _(act):
            def copy_high(b, par, kind, h):
                bank, number = place(b - 1, (kind, h))
                act.wait_ge(work_filled, number + 1)
                hi = {"xT": xT_hi, "q": qT_hi, "v": v_hi}[kind]
                act.copy(at(hi, par, slice(CW * h, CW * h + CW)), work_ps[:, bank, :]).then_inc(hi_ready, 1)

            def exponentials(b, i):
                act.wait_ge(biased_ready, TB * b + i + 1)
                n = P * (i + 1)
                act.activation(probs[:, i % 2, 0:n], biased[:, i % 2, 0:n], ACT.Exp, bias=neg_max[:, i:i + 1],
                               scale=-1.0, accum_out=prob_sum[:, i:i + 1]).then_inc(probs_ready, 1)

            def scale_sum(b, i):
                t = TB * b + i
                act.wait_ge(probs_ready, t + 1)
                act.activation(scaled_sum[:, i:i + 1], prob_sum[:, i:i + 1], ACT.Copy, scale=wpow_inv[:, 1:2])\
                   .then_inc(scaled_ready, 1)

            def copy_probsT(b, i):
                for h in range(i // CT + 1):
                    bank, number = probs_place(b, i, h)
                    n = P * min(CT, i + 1 - CT * h)
                    act.wait_ge(work_filled, number + 1)
                    act.copy(probsT_hi[:, i % 2, CW * h:CW * h + n], work_ps[:, bank, 0:n]).then_inc(probsT_hi_ready, 1)

            def around(b, par, nxt, final):
                for i in range(TB):
                    scale_sum(b, i)
                    if i + 1 < TB:
                        copy_probsT(b, i + 1)
                    elif not final:
                        copy_probsT(b + 1, 0)
                    if i < (HALVES if final else len(prologue)):
                        copy_high(b + 1, nxt, *prologue[i])
                    if i + 2 < TB:
                        exponentials(b, i + 2)
                        if final and i + 3 == TB:
                            act.activation(warm[:, :], norm_const[:, 0:1], ACT.Silu)
                    elif not final:
                        exponentials(b + 1, i + 2 - TB)

            act.wait_ge(const_ready, 7)
            act.activation(warm[:, :], norm_const[:, 0:1], ACT.Exp)
            act.wait_ge(ffn_w_loaded, 48)
            act.copy(wgu_in[:, :, :], wgu_int[:, :, :]).then_inc(ffn_w_float, 1)
            act.copy(wd_in[:, :], wd_int[:, :]).then_inc(ffn_w_float, 1)
            for part in prologue[:2]:
                copy_high(0, 0, *part)
            act.wait_ge(ffn_w_turned, 1)
            for g in range(2):
                act.copy(wguT_f[:, HB * g:HB * (g + 1), :].rearrange("p a n -> p (a n)"), gate_up_w_ps[g]).then_inc(ffn_w_copied, 1)
            act.copy(wdT_f[:, :], down_w_ps).then_inc(ffn_w_copied, 1)
            for part in prologue[2:4]:
                copy_high(0, 0, *part)
            exponentials(0, 0)
            for part in prologue[4:]:
                copy_high(0, 0, *part)
            exponentials(0, 1)
            copy_probsT(0, 0)
            with act.Fori(0, B - 1) as b:
                around(b, act.snap(b % 2), act.snap((b + 1) % 2), False)
            around(B - 1, (B - 1) % 2, B % 2, True)

            def copy_x2_high(c, par):
                act.wait_ge(x2T_filled, c - 1)
                act.copy(x2T_hi[:, par, :], x2T_ps).then_inc(x2T_hi_ready, 1)

            def silus(c, par):
                for j in range(HB):
                    act.wait_ge(gate_up_ready, HB * c + j + 1)
                    act.activation(silu[:, par, j, :], gate_ps[j], ACT.Silu, scale=gate_scale[:, 0:1]).then_inc(silu_ready, 1)

            def hidden_high(c, par):
                for j in range(HB):
                    act.wait_ge(hidden_ready, HB * c + j + 1)
                    act.copy(hidden_hi[:, par, j, :], hidden[:, par, j, :]).then_inc(hidden_hi_ready, 1)

            def pair(c, final):
                for par in range(2):
                    silus(c + par, par)
                    if not final:
                        copy_x2_high(c + par + 2, par)
                    hidden_high(c + par, par)

            with act.Fori(0, NCH // 2 - 1) as m:
                pair(2 * m, False)
            pair(NCH - 2, True)


_INS = ['L0_attn_x', 'L0_attn_W_qk', 'L0_attn_W_v', 'L0_attn_alibi_slope', 'L0_ffn_w_gate', 'L0_ffn_w_up', 'L0_ffn_w_down']


def kernel(**inputs):
    import numpy as _np
    import concourse.bacc as _bacc
    from concourse import mybir as _mybir
    from concourse.bass_utils import run_bass_kernel_spmd as _run

    nc = _bacc.Bacc("TRN2", target_bir_lowering=False, num_devices=1)
    arrays, args = {}, []
    for name in _INS:
        a = _np.ascontiguousarray(inputs[name])
        arrays[f"in_{name}_dram"] = a
        args.append(nc.dram_tensor(f"in_{name}_dram", a.shape, _mybir.dt.from_np(a.dtype), kind="ExternalInput").ap())
    shape = inputs['L0_attn_x'].shape
    args.append(nc.dram_tensor("out_0_dram", shape, _mybir.dt.float32, kind="ExternalOutput").ap())
    preln_block(nc, *args)
    r = _run(nc, [arrays], core_ids=[0])
    return r.results[0]["out_0_dram"]
```

```python
from contextlib import ExitStack

import concourse.bass as bass
from concourse import mybir

ALU = mybir.AluOpType
ACT = mybir.ActivationFunctionType
F32 = mybir.dt.float32
F16 = mybir.dt.float16
I32 = mybir.dt.int32
U32 = mybir.dt.uint32
AX_X = mybir.AxisListType.X
ds = bass.ds

P = 128
EPS = 1e-5
DEQUANT = 1.0 / 127.0
EXPONENT_BITS = 0x7F800000
F16_EXACT = 1024.0
HIDDEN_UNIT = 32.0
MASKED = -3.0e38


def preln_block(nc, x, w_qk, w_v, slope, w_gate, w_up, w_down, out):
    B, S, D = x.shape
    HID = w_gate.shape[0]
    TB = S // P
    NT = B * TB
    HB = HID // P
    CT = 4
    CW = CT * P
    NCH = NT // CT
    HALVES = S // CW
    SCALE = float(D) ** -0.5
    assert D == P and S == 2 * CW and HID % P == 0

    NWORK = 3
    EARLY = 2
    prologue = [(kind, h) for kind in ("xT", "q", "v") for h in range(HALVES)]
    probs_groups = [[(i, h) for h in range(i // CT + 1)] for i in range(TB)]
    opening = prologue + [(0, 0)]
    middle, closing = [], []

    def parts_at(i, last):
        return prologue[:HALVES if last else None][i - 1:i] if i else []

    for i in range(TB):
        middle += probs_groups[(i + 1) % TB] + parts_at(i, False)
        if i + 1 < TB:
            closing += probs_groups[i + 1]
        closing += parts_at(i, True)
    assert len(middle) % NWORK == 0

    def place(around, group):
        if isinstance(around, int) and around < 0:
            n = opening.index(group)
            return n % NWORK, n
        n = len(opening) + (closing if isinstance(around, int) and around == B - 1 else middle).index(group)
        return n % NWORK, around * len(middle) + n

    def probs_place(b, i, h):
        return place(b if i else b - 1, (i, h))

    def by_pool(group):
        return group[0] in ("xT", "q")

    def emptied(around, index):
        if isinstance(around, int) and around < 0:
            return False, index + 1
        groups = closing if isinstance(around, int) and around == B - 1 else middle
        pool_takes = index >= 0 and by_pool(groups[index])
        if index >= 0:
            n = sum(by_pool(g) == pool_takes for g in groups[:index + 1])
        else:
            n = index + 1
        per_round = sum(by_pool(g) == pool_takes for g in middle)
        return pool_takes, around * per_round + (0 if pool_takes else len(opening)) + n

    assert not any(by_pool(g) for g in middle[-NWORK:] + opening[-NWORK:])
    VECTOR_TAKES, POOL_TAKES = (len(opening) * (1 - k) + (B - 1) * sum(by_pool(g) == k for g in middle)
                                + sum(by_pool(g) == k for g in closing) for k in (False, True))
    assert middle[-1] == opening[-1] == (0, 0)

    def at(buffer, half, columns):
        if isinstance(half, int):
            return buffer[:, half, columns]
        return buffer[:, ds(half, 1), columns].rearrange("p a n -> p (a n)")

    with ExitStack() as ctx:
        def sb(name, shape, dt):
            return ctx.enter_context(nc.sbuf_tensor(name, shape, dt))

        def sem(name):
            return ctx.enter_context(nc.semaphore(name))

        wqk_in = sb("wqk_in", [P, D], F32)
        wv_in = sb("wv_in", [P, D], F32)
        wgu_int = sb("wgu_int", [P, 2 * HB, D], I32)
        wd_int = sb("wd_int", [P, HID], I32)
        wgu_in = sb("wgu_in", [P, 2 * HB, D], F32)
        wd_in = sb("wd_in", [P, HID], F32)
        slope_col = sb("slope_col", [P, 1], F32)
        ident = sb("ident", [P, P], F32)
        ones2 = sb("ones2", [2, P], F32)
        warm = sb("warm", [P, 1], F32)
        wmax = sb("wmax", [P, 4], F32)
        wmax_row = sb("wmax_row", [2, 2], F32)
        wpow_row = sb("wpow_row", [2, 2], F32)
        wpow_diag = sb("wpow_diag", [2, 2, 2], F32)
        wpow = sb("wpow", [P, 4], F32)
        wpow_inv = sb("wpow_inv", [P, 4], F32)
        int_scale = sb("int_scale", [P, 2], F32)
        int_unscale = sb("int_unscale", [P, 2], F32)
        min_int_scale = sb("min_int_scale", [1, 1], F32)
        gu_square = sb("gu_square", [P, 1], F32)
        gu_inv_square = sb("gu_inv_square", [P, 1], F32)
        hidden_scale = sb("hidden_scale", [P, 1], F32)
        gate_scale = sb("gate_scale", [P, 1], F32)
        ffn_scale = sb("ffn_scale", [P, 1], F32)
        score_scale = sb("score_scale", [P, 1], F32)
        neg_score_scale = sb("neg_score_scale", [P, 1], F32)
        score_inv = sb("score_inv", [P, 1], F32)
        slope_scaled = sb("slope_scaled", [P, 1], F32)
        distance = sb("distance", [P, S], F32)
        mask = sb("mask", [P, P], F32)
        bias = sb("bias", [P, S], F32)
        wtmp = sb("wtmp", [P, 2, D], F32)
        wqk = sb("wqk", [P, 2, D], F16)
        wvT = sb("wvT", [P, 2, D], F16)
        wguT_f = sb("wguT_f", [P, 2 * HB, P], F32)
        wguT = sb("wguT", [P, 2, 2 * HB, P], F16)
        wdT_f = sb("wdT_f", [P, HB * D], F32)
        wdT = sb("wdT", [P, 2, HB, D], F16)
        split_flag = sb("split_flag", [1, 1], I32)
        norm_const = sb("norm_const", [P, 5], F32)

        xs = sb("xs", [P, NT, D], F32)
        stats = sb("stats", [P, 2, TB, 6], F32)
        mean_sum = sb("mean_sum", [P, TB], F32)
        mean_dif = sb("mean_dif", [P, TB], F32)
        dif_sq = sb("dif_sq", [P, TB], F32)
        square_sum = sb("square_sum", [P, TB], F32)
        between = sb("between", [P, TB], F32)
        within = sb("within", [P, TB], F32)
        within_eps = sb("within_eps", [P, TB], F32)
        mean = sb("mean", [P, 2, TB], F32)
        var_eps = sb("var_eps", [P, TB], F32)
        rstd = sb("rstd", [P, 2, TB], F32)
        centred = sb("centred", [P, TB, D], F32)
        xn = sb("xn", [P, TB, D], F32)
        whole = sb("whole", [P, 4, CW], F32)
        xT_hi = sb("xT_hi", [P, 2, S], F16)
        xT_lo = sb("xT_lo", [P, 2, S], F16)
        qT_hi = sb("qT_hi", [P, 2, S], F16)
        qT_lo = sb("qT_lo", [P, 2, S], F16)
        v_hi = sb("v_hi", [P, 2, S], F16)
        v_lo = sb("v_lo", [P, 2, S], F16)
        biased = sb("biased", [P, 2, S], F32)
        probs = sb("probs", [P, 2, S], F32)
        probsT_hi = sb("probsT_hi", [P, 2, S], F16)
        probsT_lo = sb("probsT_lo", [P, 2, S], F16)
        neg_max = sb("neg_max", [P, TB], F32)
        prob_sum = sb("prob_sum", [P, TB], F32)
        scaled_sum = sb("scaled_sum", [P, TB], F32)
        inv_sum = sb("inv_sum", [P, TB], F32)
        silu = sb("silu", [P, 2, HB, CW], F32)
        hidden = sb("hidden", [P, 2, HB, CW], F32)
        x2T_hi, x2T_lo = (part[:, B % 2, :].rearrange("p (c n) -> p c n", c=2) for part in (xT_hi, xT_lo))
        hidden_hi = sb("hidden_hi", [P, 2, HB, CW], F16)
        hidden_lo = sb("hidden_lo", [P, 2, HB, CW], F16)

        score_ps = ctx.enter_context(nc.psum_tensor("score_ps", [P, 2, S], F32))
        attn_ps = ctx.enter_context(nc.psum_tensor("attn_ps", [P, 512], F32))
        work_ps = ctx.enter_context(nc.psum_tensor("work_ps", [P, NWORK, 512], F32))
        gate_ps = [score_ps[:, 0, 0:CW], score_ps[:, 1, 0:CW], work_ps[:, 0, :]]
        up_ps = [score_ps[:, 0, CW:S], score_ps[:, 1, CW:S], work_ps[:, 1, :]]
        x2T_ps = work_ps[:, 2, :]
        gate_up_w_ps = [score_ps[:, 0, CW:CW + HID], score_ps[:, 1, CW:CW + HID]]
        down_w_ps = score_ps[:, 1, 0:HID]
        v_w_ps = score_ps[:, 0, 0:D]
        down_ps = attn_ps[:, :]
        last_ps = gate_ps[0:2]
        last_halves = [range(0, CT // 2), range(CT // 2, CT)]

        x_loaded = [sem(f"x_loaded{b}") for b in range(B)]
        attn_w_loaded = sem("attn_w_loaded")
        ffn_w_loaded = sem("ffn_w_loaded")
        slope_loaded = sem("slope_loaded")
        first_half_loaded = sem("first_half_loaded")
        const_ready = sem("const_ready")
        ident_ready = sem("ident_ready")
        w_step = sem("w_step")
        w_max_ready = sem("w_max_ready")
        w_max_turned = sem("w_max_turned")
        w_diag_ready = sem("w_diag_ready")
        w_pow_spread = sem("w_pow_spread")
        w_pow_copied = sem("w_pow_copied")
        wv_turned = sem("wv_turned")
        ffn_w_float = sem("ffn_w_float")
        ffn_w_turned = sem("ffn_w_turned")
        ffn_w_copied = sem("ffn_w_copied")
        attn_w_ready = sem("attn_w_ready")
        int_scale_ready = sem("int_scale_ready")
        ffn_w_scaled = sem("ffn_w_scaled")
        ffn_w_hi_ready = sem("ffn_w_hi_ready")
        split_flag_ready = sem("split_flag_ready")
        ffn_w_ready = sem("ffn_w_ready")
        distance_ready = sem("distance_ready")
        mask_ready = sem("mask_ready")
        slope_ready = sem("slope_ready")
        bias_ready = sem("bias_ready")
        stats_done = sem("stats_done")
        pool_step = sem("pool_step")
        xn_ready = sem("xn_ready")
        first_half_ready = sem("first_half_ready")
        work_filled = sem("work_filled")
        work_emptied = sem("work_emptied")
        work_copied = sem("work_copied")
        copied_split = sem("copied_split")
        hi_ready = sem("hi_ready")
        probsT_hi_ready = sem("probsT_hi_ready")
        scores_ready = sem("scores_ready")
        biased_ready = sem("biased_ready")
        probs_ready = sem("probs_ready")
        attn_ready = sem("attn_ready")
        scaled_ready = sem("scaled_ready")
        inv_ready = sem("inv_ready")
        attn_added = sem("attn_added")
        x2T_filled = sem("x2T_filled")
        x2T_hi_ready = sem("x2T_hi_ready")
        x2T_ready = sem("x2T_ready")
        gate_up_ready = sem("gate_up_ready")
        silu_ready = sem("silu_ready")
        hidden_ready = sem("hidden_ready")
        hidden_hi_ready = sem("hidden_hi_ready")
        pool_lo_ready = sem("pool_lo_ready")
        vector_lo_ready = sem("vector_lo_ready")
        down_ready = sem("down_ready")
        result_ready = sem("result_ready")
        stored = sem("stored")

        N_CONST = 8
        N_READ, N_SMALL = 3, 10
        N_STEPS = N_SMALL + HALVES

        def apart(n):
            return int(isinstance(n, int) and n in (0, B + 3))

        def steps_before(n):
            return N_STEPS * n - 1 if not (isinstance(n, int) and n == 0) else 0

        block = ctx.enter_context(nc.Block())

        def pool_blocks(c):
            return 0 if isinstance(c, int) and c == 0 else 1 if isinstance(c, int) and c == NCH - 1 else HB - 1

        def pool_blocks_to(c):
            return (HB - 1) * c - (1 if isinstance(c, int) and c == NCH - 1 else 0)

        def vector_blocks_to(c):
            return HB + c + (1 if isinstance(c, int) and c == NCH - 1 else 0)

        def copied_before(b, kind, h):
            return sum(by_pool(g) for g in prologue) * (b - 1) + prologue.index((kind, h))

        @block.sync
        def _(sp):
            xv = x.rearrange("b (j p) d -> b p j d", p=P)
            ov = out.rearrange("b (j p) d -> p (b j) d", p=P)
            for h in range(HALVES):
                tiles = slice(CT * h, CT * (h + 1))
                sp.dma_start(xs[:, tiles, :], xv[0][:, tiles, :]).then_inc(x_loaded[0] if h else first_half_loaded, 16)
            sp.dma_start(wqk_in[:, :], w_qk).then_inc(attn_w_loaded, 16)
            sp.dma_start(wv_in[:, :], w_v).then_inc(attn_w_loaded, 16)
            sp.dma_start(wgu_int[:, 0:HB, :], w_gate.rearrange("(j p) d -> p j d", p=P)).then_inc(ffn_w_loaded, 16)
            sp.dma_start(wgu_int[:, HB:2 * HB, :], w_up.rearrange("(j p) d -> p j d", p=P)).then_inc(ffn_w_loaded, 16)
            sp.dma_start(wd_int[:, :], w_down).then_inc(ffn_w_loaded, 16)
            sp.dma_start(slope_col[:, :], slope.rearrange("(a d) -> a d", a=1).broadcast_to([P, 1]))\
              .then_inc(slope_loaded, 16)
            for b in range(1, B):
                sp.dma_start(xs[:, TB * b:TB * (b + 1), :], xv[b]).then_inc(x_loaded[b], 16)
            with sp.Fori(0, NCH - 1) as c:
                sp.wait_ge(result_ready, c + 1)
                sp.dma_start(ov[:, ds(CT * c, CT), :], xs[:, ds(CT * c, CT), :]).then_inc(stored, 16)
            for k, half in enumerate(last_halves):
                tiles = slice(CT * (NCH - 1) + half[0], CT * (NCH - 1) + half[-1] + 1)
                sp.wait_ge(result_ready, NCH + k)
                sp.dma_start(ov[:, tiles, :], xs[:, tiles, :]).then_inc(stored, 16)
            sp.wait_ge(stored, 16 * (NCH + 1))

        @block.gpsimd
        def _(pool):
            pool.memset(ident[:, :], 0.0).then_inc(const_ready, 1)
            pool.memset(mask[:, :], 0.0).then_inc(const_ready, 1)
            pool.memset(ones2[:, :], 1.0).then_inc(const_ready, 1)
            for n, value in enumerate((0.5, 0.25, 1.0 / D, EPS, -0.5)):
                pool.memset(norm_const[:, n:n + 1], value).then_inc(const_ready, 1)
            pool.wait_ge(const_ready, N_CONST)
            pool.affine_select(out=ident[:, :], in_=ident[:, :], compare_op=ALU.not_equal, fill=1.0, base=0,
                               pattern=[[-1, P]], channel_multiplier=1).then_inc(ident_ready, 1)
            pool.iota(distance[:, :], pattern=[[1, S]], base=P - S, channel_multiplier=-1,
                      allow_small_or_imprecise_dtypes=True).then_inc(distance_ready, 1)
            pool.affine_select(out=mask[:, :], in_=mask[:, :], compare_op=ALU.is_ge, fill=MASKED, base=0,
                               pattern=[[-1, P]], channel_multiplier=1).then_inc(mask_ready, 1)

            def tiles_of(n, h):
                return xs[:, ds(TB * (n % B) + CT * h, CT), :]

            def per_row(column, t):
                return column[:, t].rearrange("p (t a) -> p t a", a=1).broadcast_to([P, CT, D])

            def halves_of(n):
                return range(int(isinstance(n, int) and n == 0), HALVES)

            def moments(n):
                steps, stat = steps_before(n), stats[:, apart(n), :, :]
                half, quarter, per_element, eps, power = (norm_const[:, k:k + 1].broadcast_to([P, TB]) for k in range(5))

                def small(out, a, b, op):
                    pool.tensor_tensor(out, a, b, op).then_inc(pool_step, 1)

                pool.wait_ge(stats_done, n + 1)
                small(mean_sum[:, :], stat[:, :, 1], stat[:, :, 4], ALU.add)
                small(mean_dif[:, :], stat[:, :, 1], stat[:, :, 4], ALU.subtract)
                small(square_sum[:, :], stat[:, :, 2], stat[:, :, 5], ALU.add)
                pool.wait_ge(pool_step, steps + N_READ)
                small(mean[:, apart(n), :], mean_sum[:, :], half, ALU.mult)
                small(dif_sq[:, :], mean_dif[:, :], mean_dif[:, :], ALU.mult)
                small(within[:, :], square_sum[:, :], per_element, ALU.mult)
                pool.wait_ge(pool_step, steps + 6)
                small(between[:, :], dif_sq[:, :], quarter, ALU.mult)
                small(within_eps[:, :], within[:, :], eps, ALU.add)
                pool.wait_ge(pool_step, steps + 8)
                small(var_eps[:, :], within_eps[:, :], between[:, :], ALU.add)
                pool.wait_ge(pool_step, steps + 9)
                small(rstd[:, apart(n), :], var_eps[:, :], power, ALU.pow)

            def centre(n):
                pool.wait_ge(pool_step, steps_before(n) + 4)
                if isinstance(n, int) and n == B + 3:
                    pool.wait_ge(xn_ready, HALVES * n - 1)
                for h in halves_of(n):
                    t = slice(CT * h, CT * h + CT)
                    pool.tensor_tensor(centred[:, t, :], tiles_of(n, h), per_row(mean[:, apart(n), :], t), ALU.subtract)\
                        .then_inc(pool_step, 1)

            def scale(n):
                if isinstance(n, int) and n > B + 1:
                    pool.wait_ge(x2T_filled, HALVES * (n - B - 1))
                elif not (isinstance(n, int) and n == 0):
                    pool.wait_ge(work_filled, place(n - 2, ("xT", HALVES - 1))[1] + 1)
                for k, h in enumerate(halves_of(n)):
                    t = slice(CT * h, CT * h + CT)
                    pool.wait_ge(pool_step, steps_before(n) + N_SMALL + k + 1)
                    pool.tensor_tensor(xn[:, t, :], centred[:, t, :], per_row(rstd[:, apart(n), :], t), ALU.mult)\
                        .then_inc(xn_ready, 1)

            def norm(n):
                moments(n)
                centre(n)
                scale(n)

            def hidden_low(c, par):
                for j in range(pool_blocks(c)):
                    pool.wait_ge(hidden_hi_ready, HB * c + j + 1)
                    pool.tensor_tensor(hidden_lo[:, par, j, :], hidden[:, par, j, :], hidden_hi[:, par, j, :],
                                       ALU.subtract).then_inc(pool_lo_ready, 1)

            norm(0)
            pool.wait_ge(distance_ready, 1)
            pool.wait_ge(mask_ready, 1)
            pool.wait_ge(slope_ready, 1)
            for k, keys in enumerate((slice(CW, S), slice(0, CW))):
                pool.tensor_tensor(bias[:, keys], distance[:, keys], slope_scaled[:, 0:1].broadcast_to([P, CW]), ALU.mult)\
                    .then_inc(bias_ready, 1)
                if k == 0:
                    pool.wait_ge(bias_ready, 1)
                    pool.tensor_tensor(bias[:, S - P:S], bias[:, S - P:S], mask[:, :], ALU.add).then_inc(bias_ready, 1)
            norm(1)
            pool.wait_ge(ffn_w_hi_ready, 1)
            pool.tensor_tensor(wguT[:, 1, :, :], wguT_f[:, :, :], wguT[:, 0, :, :], ALU.subtract).then_inc(ffn_w_ready, 1)
            pool.tensor_tensor(wdT[:, 1, :, :].rearrange("p a n -> p (a n)"), wdT_f[:, :],
                               wdT[:, 0, :, :].rearrange("p a n -> p (a n)"), ALU.subtract).then_inc(ffn_w_ready, 1)

            def split_low(b, par, kind, h):
                hi, lo = {"xT": (xT_hi, xT_lo), "q": (qT_hi, qT_lo)}[kind]
                cols = slice(CW * h, CW * h + CW)
                pool.wait_ge(work_copied, copied_before(b, kind, h) + 1)
                pool.tensor_tensor(at(lo, par, cols), whole[:, prologue.index((kind, h)), :], at(hi, par, cols),
                                   ALU.subtract).then_inc(copied_split, 1)

            with pool.Fori(0, B - 1) as b:
                nxt = pool.snap((b + 1) % 2)
                for part in prologue:
                    if by_pool(part):
                        split_low(b + 1, nxt, *part)
                norm(b + 2)
            for part in prologue[:HALVES]:
                split_low(B, B % 2, *part)
            norm(B + 1)
            moments(B + 2)
            centre(B + 2)
            moments(B + 3)
            scale(B + 2)
            hidden_low(1, 1)
            centre(B + 3)
            hidden_low(2, 0)
            scale(B + 3)
            hidden_low(3, 1)
            with pool.Fori(2, NCH // 2 - 1) as m:
                for par in range(2):
                    hidden_low(2 * m + par, par)
            for par in range(2):
                hidden_low(NCH - 2 + par, par)

        @block.tensor
        def _(pe):
            def turn_maxima(pair):
                pe.wait_ge(w_max_ready, pair + 1)
                if pair:
                    pe.wait_ge(w_pow_copied, pair)
                pe.transpose(attn_ps[0:2, 0:P], wmax[:, 2 * pair:2 * pair + 2], ident[:, :]).then_inc(w_max_turned, 1)

            def spread_powers(pair):
                pe.wait_ge(w_diag_ready, pair + 1)
                pe.matmul(attn_ps[:, 256:258], ones2[:, :], wpow_diag[:, pair, :], start=True, stop=True)\
                  .then_inc(w_pow_spread, 1)

            def wait_emptied(around, index, split=False):
                copied, count = emptied(around, index)
                pe.wait_ge(work_emptied if not copied else copied_split if split else work_copied, count)

            def index_of(around, group):
                if isinstance(around, int) and around < 0:
                    return opening.index(group)
                return (closing if isinstance(around, int) and around == B - 1 else middle).index(group)

            def fill(around, group, emit):
                index = index_of(around, group)
                if not (isinstance(around, int) and around < 0 and index < NWORK):
                    wait_emptied(around, index - NWORK)
                emit(work_ps[:, place(around, group)[0], :]).then_inc(work_filled, 1)

            def taken(around, group):
                wait_emptied(around, index_of(around, group), split=True)

            def three(o, left, right):
                (l_hi, l_lo), (r_hi, r_lo) = left, right
                pe.matmul(o, l_hi, r_hi, start=True, stop=False)
                pe.matmul(o, l_hi, r_lo, start=False, stop=False)
                return pe.matmul(o, l_lo, r_hi, start=False, stop=True)

            def prologue_part(b, par, kind, h):
                cols = slice(CW * h, CW * h + CW)

                def transpose_x(ps):
                    for j in range(CT):
                        m = pe.transpose(ps[:, P * j:P * (j + 1)], xn[:, CT * h + j, :], ident[:, :])
                    return m

                def project_q(ps):
                    return three(ps, (wqk[:, 0, :], wqk[:, 1, :]), (at(xT_hi, par, cols), at(xT_lo, par, cols)))

                def project_v(ps):
                    for j in range(CT):
                        tok = slice(CW * h + P * j, CW * h + P * j + P)
                        m = three(ps[:, P * j:P * j + P], (at(xT_hi, par, tok), at(xT_lo, par, tok)),
                                  (wvT[:, 0, :], wvT[:, 1, :]))
                    return m

                if kind == "xT":
                    if isinstance(b, int) and (b, h) == (0, 0):
                        pe.wait_ge(first_half_ready, 1)
                    else:
                        pe.wait_ge(xn_ready, HALVES * b + h)
                else:
                    taken(b - 1, ("xT", h))
                fill(b - 1, (kind, h), {"xT": transpose_x, "q": project_q, "v": project_v}[kind])

            def scores(b, par, i):
                t = TB * b + i
                if i in (0, 2):
                    taken(b - 1, ("q", i // 2))
                if not (isinstance(t, int) and t < 2):
                    pe.wait_ge(biased_ready, t - 1)
                rows = slice(P * i, P * (i + 1))
                for k0 in range(0, P * (i + 1), CW):
                    keys = slice(k0, min(k0 + CW, P * (i + 1)))
                    m = three(score_ps[:, i % 2, keys], (at(qT_hi, par, rows), at(qT_lo, par, rows)),
                              (at(xT_hi, par, keys), at(xT_lo, par, keys)))
                m.then_inc(scores_ready, 1)

            def transpose_probs(b, i):
                pe.wait_ge(probs_ready, TB * b + i + 1)
                for h in range(i // CT + 1):
                    def emit(ps, h=h):
                        for j in range(min(CT, i + 1 - CT * h)):
                            k0 = CW * h + P * j
                            m = pe.transpose(ps[:, P * j:P * (j + 1)], probs[:, i % 2, k0:k0 + P], ident[:, :])
                        return m
                    fill(b if i else b - 1, (i, h), emit)

            def weigh_values(b, par, i):
                if i == 0:
                    wait_emptied(b, -1)
                else:
                    taken(b, (i, i // CT))
                pe.wait_ge(attn_added, TB * b + i)
                for j in range(i + 1):
                    keys = slice(P * j, P * (j + 1))
                    p_hi, p_lo = probsT_hi[:, i % 2, keys], probsT_lo[:, i % 2, keys]
                    v_j = at(v_hi, par, keys)
                    pe.matmul(attn_ps[:, 0:D], p_hi, v_j, start=(j == 0), stop=False)
                    pe.matmul(attn_ps[:, 0:D], p_hi, at(v_lo, par, keys), start=False, stop=False)
                    m = pe.matmul(attn_ps[:, 0:D], p_lo, v_j, start=False, stop=(j == i))
                m.then_inc(attn_ready, 1)

            def by_int_parts(product):
                with pe.If(needs_lo == 1):
                    product(True)
                with pe.Else():
                    product(False)

            def gate_up(c, par, blocks=range(HB)):
                def product(with_lo):
                    if not (isinstance(c, int) and c < 2):
                        pe.wait_ge(x2T_ready, c - 1)
                    for j in blocks:
                        if not (isinstance(c, int) and c == 0):
                            pe.wait_ge(hidden_ready, HB * (c - 1) + j + 1)
                        for o, w in ((gate_ps[j], j), (up_ps[j], HB + j)):
                            pe.matmul(o, wguT[:, 0, w, :], x2T_hi[:, par, :], start=True, stop=False)
                            if with_lo:
                                pe.matmul(o, wguT[:, 1, w, :], x2T_hi[:, par, :], start=False, stop=False)
                            m = pe.matmul(o, wguT[:, 0, w, :], x2T_lo[:, par, :], start=False, stop=True)
                        m.then_inc(gate_up_ready, 1)

                by_int_parts(product)

            def around(b, par, nxt, final):
                for i in range(TB):
                    if i + 3 < TB:
                        scores(b, par, i + 3)
                    elif not final:
                        scores(b + 1, nxt, i + 3 - TB)
                    if i + 1 < TB:
                        transpose_probs(b, i + 1)
                    elif not final:
                        transpose_probs(b + 1, 0)
                    for part in parts_at(i, final):
                        prologue_part(b + 1, nxt, *part)
                    if final and i >= TB - EARLY:
                        j = i - (TB - EARLY)
                        if j == 0:
                            pe.wait_ge(ffn_w_ready, 2)
                            pe.wait_ge(copied_split, POOL_TAKES)
                        pe.wait_ge(biased_ready, NT - EARLY + 1 + j)
                        gate_up(0, 0, [j])
                    weigh_values(b, par, i)

            def keep_busy(n):
                for _ in range(n):
                    pe.transpose(work_ps[:, NWORK - 1, 0:P], ident[:, :], ident[:, :])

            pe.wait_ge(ident_ready, 1)
            pe.wait_ge(attn_w_loaded, 32)
            pe.transpose(v_w_ps, wv_in[:, :], ident[:, :]).then_inc(wv_turned, 1)
            turn_maxima(0)
            spread_powers(0)
            pe.wait_ge(ffn_w_float, 2)
            for j in range(2 * HB):
                pe.transpose(gate_up_w_ps[j // HB][:, P * (j % HB):P * (j % HB + 1)], wgu_in[:, j, :], ident[:, :])
            for j in range(HB):
                m = pe.transpose(down_w_ps[:, P * j:P * (j + 1)], wd_in[:, P * j:P * (j + 1)], ident[:, :])
            m.then_inc(ffn_w_turned, 1)
            turn_maxima(1)
            keep_busy(3)
            prologue_part(0, 0, *prologue[0])
            spread_powers(1)
            prologue_part(0, 0, *prologue[1])
            keep_busy(4)
            pe.wait_ge(attn_w_ready, 1)
            prologue_part(0, 0, *prologue[2])
            prologue_part(0, 0, *prologue[3])
            pe.wait_ge(ffn_w_copied, 3)
            scores(0, 0, 0)
            scores(0, 0, 1)
            prologue_part(0, 0, *prologue[4])
            scores(0, 0, 2)
            prologue_part(0, 0, *prologue[5])
            transpose_probs(0, 0)
            pe.wait_ge(w_pow_copied, 2)
            with pe.Fori(0, B - 1) as b:
                around(b, pe.snap(b % 2), pe.snap((b + 1) % 2), False)
            pe.wait_ge(split_flag_ready, 1)
            needs_lo = pe.value_load(split_flag[0:1, 0:1], min_val=0, max_val=1)
            around(B - 1, (B - 1) % 2, B % 2, True)

            pe.wait_ge(work_emptied, VECTOR_TAKES)

            def transpose_x2(c, par):
                pe.wait_ge(xn_ready, HALVES * B + c)
                if not (isinstance(c, int) and c == 2):
                    pe.wait_ge(x2T_ready, c - 2)
                for j in range(CT):
                    m = pe.transpose(x2T_ps[:, P * j:P * (j + 1)], xn[:, CT * par + j, :], ident[:, :])
                m.then_inc(x2T_filled, 1)

            def down(c, par, o=down_ps, tiles=range(CT)):
                def product(with_lo):
                    if not (isinstance(c, int) and c == 0):
                        pe.wait_ge(pool_lo_ready, pool_blocks_to(c))
                    pe.wait_ge(vector_lo_ready, vector_blocks_to(c))
                    if isinstance(c, int) and c == 0:
                        pe.wait_ge(attn_added, NT)
                    elif not (isinstance(c, int) and c == NCH - 1):
                        pe.wait_ge(result_ready, c)
                    for j in tiles:
                        for k in range(HB):
                            h_hi, h_lo = (h[:, par, k, P * j:P * (j + 1)] for h in (hidden_hi, hidden_lo))
                            w_hi, w_lo = wdT[:, 0, k, :], wdT[:, 1, k, :]
                            cols = slice(P * (j - tiles[0]), P * (j - tiles[0] + 1))
                            pe.matmul(o[:, cols], h_hi, w_hi, start=(k == 0), stop=False)
                            if with_lo:
                                pe.matmul(o[:, cols], h_hi, w_lo, start=False, stop=False)
                            m = pe.matmul(o[:, cols], h_lo, w_hi, start=False, stop=(k == HB - 1))
                    m.then_inc(down_ready, 1)

                by_int_parts(product)

            def pair(c, first, final):
                for par in range(2):
                    gate_up(c + par, par, range(EARLY if first and par == 0 else 0, HB))
                    if not final:
                        transpose_x2(c + par + 2, par)
                    if not (first and par == 0):
                        down(c + par - 1, 1 - par)

            pair(0, True, False)
            with pe.Fori(1, NCH // 2 - 1) as m:
                pair(2 * m, False, False)
            pair(NCH - 2, False, True)
            for half, o in zip(last_halves, last_ps):
                down(NCH - 1, 1, o, half)

        @block.vector
        def _(dve):
            step = [0]
            def link(ins):
                step[0] += 1
                ins.then_inc(w_step, 1)
                dve.wait_ge(w_step, step[0])

            def statistics(n, j):
                if j == 0 and not (isinstance(n, int) and n in (0, 1, B + 3)):
                    dve.wait_ge(pool_step, steps_before(n) - N_STEPS + N_READ)
                m = dve.bn_stats(stats[:, apart(n), j, :], at(xs, TB * (n % B) + j, slice(0, D)))
                if j == TB - 1:
                    m.then_inc(stats_done, 1)

            def normalise_first_half():
                dve.wait_ge(pool_step, N_SMALL)
                for j in range(CT):
                    m = dve.tensor_scalar(xn[:, j, :], xs[:, j, :], mean[:, 1, j:j + 1], rstd[:, 1, j:j + 1],
                                          ALU.subtract, ALU.mult)
                m.then_inc(first_half_ready, 1)

            def offer_maxima(pair, least):
                cols = slice(2 * pair, 2 * pair + 2)
                dve.tensor_scalar(wmax[:, cols], wmax[:, cols], least, None, ALU.max).then_inc(w_max_ready, 1)

            def take_exponents(pair):
                dve.wait_ge(w_max_turned, pair + 1)
                link(dve.tensor_reduce(wmax_row[:, pair:pair + 1], attn_ps[0:2, 0:P], AX_X, ALU.max))
                link(dve.tensor_scalar(wpow_row[:, pair:pair + 1].bitcast(U32), wmax_row[:, pair:pair + 1].bitcast(U32),
                                       EXPONENT_BITS, None, ALU.bitwise_and))
                dve.tensor_scalar(wpow_diag[:, pair, :], ident[0:2, 0:2], wpow_row[:, pair:pair + 1], None, ALU.mult)\
                   .then_inc(w_diag_ready, 1)

            def take_powers(pair):
                cols = slice(2 * pair, 2 * pair + 2)
                dve.wait_ge(w_pow_spread, pair + 1)
                dve.tensor_copy(wpow[:, cols], attn_ps[:, 256:258]).then_inc(w_pow_copied, 1)
                dve.wait_ge(w_pow_copied, pair + 1)
                link(dve.reciprocal(wpow_inv[:, cols], wpow[:, cols]))

            def attention_maxima():
                dve.wait_ge(attn_w_loaded, 32)
                dve.tensor_reduce(wmax[:, 0:1], wqk_in[:, :], AX_X, ALU.max, apply_absolute_value=True)
                link(dve.tensor_reduce(wmax[:, 1:2], wv_in[:, :], AX_X, ALU.max, apply_absolute_value=True))

            def attention_weights():
                dve.wait_ge(wv_turned, 1)
                link(dve.tensor_scalar(score_scale[:, :], wpow[:, 0:1], SCALE, None, ALU.mult))
                dve.tensor_scalar(wtmp[:, 0, :], wqk_in[:, :], wpow_inv[:, 0:1], None, ALU.mult)
                link(dve.tensor_scalar(wtmp[:, 1, :], v_w_ps, wpow_inv[:, 1:2], None, ALU.mult))
                dve.wait_ge(slope_loaded, 16)
                dve.reciprocal(score_inv[:, :], score_scale[:, :])
                dve.tensor_scalar(neg_score_scale[:, :], score_scale[:, :], -1.0, None, ALU.mult)
                dve.tensor_copy(wqk[:, 0, :], wtmp[:, 0, :])
                link(dve.tensor_copy(wvT[:, 0, :], wtmp[:, 1, :]))
                dve.tensor_tensor(slope_scaled[:, :], slope_col[:, :], score_inv[:, :], ALU.mult).then_inc(slope_ready, 1)
                dve.tensor_tensor(wqk[:, 1, :], wtmp[:, 0, :], wqk[:, 0, :], ALU.subtract)
                dve.tensor_tensor(wvT[:, 1, :], wtmp[:, 1, :], wvT[:, 0, :], ALU.subtract).then_inc(attn_w_ready, 1)

            def ffn_maxima():
                dve.wait_ge(ffn_w_float, 2)
                dve.tensor_reduce(wmax[:, 2:3], wgu_in[:, :, :].rearrange("p a n -> p (a n)"), AX_X, ALU.max,
                                  apply_absolute_value=True)
                link(dve.tensor_reduce(wmax[:, 3:4], wd_in[:, :], AX_X, ALU.max, apply_absolute_value=True))

            def offer_int_scale():
                dve.tensor_scalar(int_scale[:, :], wpow_inv[:, 2:4], F16_EXACT, 1.0, ALU.mult, ALU.min)\
                   .then_inc(int_scale_ready, 1)

            def ffn_scales():
                dve.wait_ge(int_scale_ready, 1)
                dve.tensor_tensor(gu_square[:, :], wpow[:, 2:3], wpow[:, 2:3], ALU.mult)
                dve.tensor_tensor(gu_inv_square[:, :], wpow_inv[:, 2:3], wpow_inv[:, 2:3], ALU.mult)
                dve.tensor_reduce(min_int_scale[0:1, :], int_scale[0:1, :], AX_X, ALU.min)
                link(dve.reciprocal(int_unscale[:, :], int_scale[:, :]))
                dve.tensor_scalar(split_flag[0:1, 0:1], min_int_scale[0:1, 0:1], 1.0, None, ALU.is_lt)\
                   .then_inc(split_flag_ready, 1)
                dve.tensor_scalar(gate_scale[:, :], int_unscale[:, 0:1], DEQUANT, None, ALU.mult)
                dve.scalar_tensor_tensor(hidden_scale[:, :], gu_inv_square[:, :], HIDDEN_UNIT, int_unscale[:, 0:1],
                                         ALU.mult, ALU.mult)
                dve.scalar_tensor_tensor(ffn_scale[:, :], gu_square[:, :], DEQUANT * DEQUANT / HIDDEN_UNIT,
                                         int_unscale[:, 1:2], ALU.mult, ALU.mult)

            def split_low(b, par, kind, h):
                bank, _ = place(b - 1, (kind, h))
                hi, lo = {"xT": (xT_hi, xT_lo), "q": (qT_hi, qT_lo), "v": (v_hi, v_lo)}[kind]
                dve.wait_ge(hi_ready, len(prologue) * b + prologue.index((kind, h)) + 1)
                cols = slice(CW * h, CW * h + CW)
                dve.tensor_tensor(at(lo, par, cols), work_ps[:, bank, :], at(hi, par, cols), ALU.subtract)\
                   .then_inc(work_emptied, 1)

            def split_probsT(b, i):
                for h in range(i // CT + 1):
                    bank, number = probs_place(b, i, h)
                    n = P * min(CT, i + 1 - CT * h)
                    cols = slice(CW * h, CW * h + n)
                    dve.wait_ge(probsT_hi_ready, (TB + TB - CT) * b + i + max(0, i - CT) + h + 1)
                    dve.tensor_tensor(probsT_lo[:, i % 2, cols], work_ps[:, bank, 0:n], probsT_hi[:, i % 2, cols],
                                      ALU.subtract).then_inc(work_emptied, 1)

            def inverse_sum(b, i, more):
                t = TB * b + i
                dve.wait_ge(scaled_ready, t + 1)
                if more:
                    dve.wait_ge(probs_ready, t + 2)
                    dve.wait_ge(scores_ready, t + 4)
                dve.reciprocal(inv_sum[:, i:i + 1], scaled_sum[:, i:i + 1]).then_inc(inv_ready, 1)

            def bias_scores(i):
                n = P * (i + 1)
                dve.tensor_tensor_reduce(biased[:, i % 2, 0:n], score_ps[:, i % 2, 0:n], bias[:, S - n:S],
                                         neg_score_scale[:, 0:1], 3.0e38, ALU.add, ALU.min, neg_max[:, i:i + 1])\
                   .then_inc(biased_ready, 1)

            def add_attention(b, i):
                t = TB * b + i
                dve.wait_ge(inv_ready, t + 1)
                dve.wait_ge(attn_ready, t + 1)
                row = xs[:, ds(t, 1), :].rearrange("p a n -> p (a n)")
                dve.scalar_tensor_tensor(row, attn_ps[:, 0:D], inv_sum[:, i:i + 1], row, ALU.mult, ALU.add)\
                   .then_inc(attn_added, 1)

            def multiply(c, par, blocks=range(HB)):
                for j in blocks:
                    dve.wait_ge(silu_ready, HB * c + j + 1)
                    if j == 0 and not (isinstance(c, int) and c < 3):
                        dve.wait_ge(pool_lo_ready, pool_blocks_to(c - 2))
                    dve.scalar_tensor_tensor(hidden[:, par, j, :], up_ps[j], hidden_scale[:, 0:1], silu[:, par, j, :],
                                             ALU.mult, ALU.mult).then_inc(hidden_ready, 1)

            def around(b, par, nxt, final):
                for i in range(TB):
                    more = i + 3 < TB or not final
                    inverse_sum(b, i, more)
                    if more:
                        bias_scores((i + 3) % TB)
                    if i + 1 < TB:
                        split_probsT(b, i + 1)
                    elif not final:
                        split_probsT(b + 1, 0)
                    for part in parts_at(i, final):
                        if not by_pool(part):
                            split_low(b + 1, nxt, *part)
                    if final and i % (TB // 2) < HALVES:
                        for j in range(CT):
                            statistics(b + 2 + i // (TB // 2), CT * (i % (TB // 2)) + j)
                    if final:
                        if i:
                            dve.wait_ge(attn_added, TB * b + i)
                            statistics(b + 4, i - 1)
                    if final and i == TB - 1:
                        multiply(0, 0, range(EARLY))
                    add_attention(b, i)
                    if not final and i < TB // 2:
                        statistics(b + 2, 2 * i)
                        statistics(b + 2, 2 * i + 1)

            for j in range(TB):
                if j % CT == 0:
                    dve.wait_ge(x_loaded[0] if j else first_half_loaded, 16)
                statistics(0, j)
            attention_maxima()
            offer_maxima(0, 1.0e-30)
            take_exponents(0)
            ffn_maxima()
            offer_maxima(1, 1.0)
            take_powers(0)
            normalise_first_half()
            take_exponents(1)
            attention_weights()
            split_low(0, 0, *prologue[0])
            take_powers(1)
            offer_int_scale()
            split_low(0, 0, *prologue[1])
            dve.wait_ge(x_loaded[1], 16)
            for j in range(TB):
                statistics(1, j)
            split_low(0, 0, *prologue[2])
            dve.wait_ge(bias_ready, 3)
            dve.wait_ge(scores_ready, 1)
            bias_scores(0)
            split_low(0, 0, *prologue[3])
            dve.wait_ge(scores_ready, 2)
            bias_scores(1)
            ffn_scales()
            split_low(0, 0, *prologue[4])
            dve.wait_ge(scores_ready, 3)
            dve.wait_ge(probs_ready, 1)
            bias_scores(2)
            split_low(0, 0, *prologue[5])
            split_probsT(0, 0)
            for b in range(2, B):
                dve.wait_ge(x_loaded[b], 16)
            with dve.Fori(0, B - 1) as b:
                around(b, dve.snap(b % 2), dve.snap((b + 1) % 2), False)
            around(B - 1, (B - 1) % 2, B % 2, True)

            def split_x2(c, par):
                dve.wait_ge(x2T_hi_ready, c - 1)
                dve.tensor_tensor(x2T_lo[:, par, :], x2T_ps, x2T_hi[:, par, :], ALU.subtract).then_inc(x2T_ready, 1)

            def add_ffn(c):
                dve.wait_ge(down_ready, c + 1)
                rows = xs[:, ds(CT * c, CT), :].rearrange("p a n -> p (a n)")
                dve.scalar_tensor_tensor(rows, down_ps, ffn_scale[:, 0:1], rows, ALU.mult, ALU.add)\
                   .then_inc(result_ready, 1)

            def hidden_low(c, par):
                for j in range(pool_blocks(c), HB):
                    dve.wait_ge(hidden_hi_ready, HB * c + j + 1)
                    dve.tensor_tensor(hidden_lo[:, par, j, :], hidden[:, par, j, :], hidden_hi[:, par, j, :],
                                      ALU.subtract).then_inc(vector_lo_ready, 1)

            def pair(c, first, final):
                for par in range(2):
                    multiply(c + par, par, range(EARLY if first and par == 0 else 0, HB))
                    if not final:
                        split_x2(c + par + 2, par)
                    last = final and par == 1
                    if last:
                        hidden_low(c + par, par)
                    if not (first and par == 0):
                        add_ffn(c + par - 1)
                    if not last:
                        hidden_low(c + par, par)

            dve.wait_ge(attn_added, NT)
            statistics(B + 3, TB - 1)
            pair(0, True, False)
            with dve.Fori(1, NCH // 2 - 1) as m:
                pair(2 * m, False, False)
            pair(NCH - 2, False, True)
            for k, (half, o) in enumerate(zip(last_halves, last_ps)):
                dve.wait_ge(down_ready, NCH + k)
                n = P * len(half)
                rows = xs[:, CT * (NCH - 1) + half[0]:CT * (NCH - 1) + half[-1] + 1, :].rearrange("p a n -> p (a n)")
                dve.scalar_tensor_tensor(rows, o[:, 0:n], ffn_scale[:, 0:1], rows, ALU.mult, ALU.add)\
                   .then_inc(result_ready, 1)

        @block.scalar
        def _(act):
            def copy_high(b, par, kind, h):
                bank, number = place(b - 1, (kind, h))
                act.wait_ge(work_filled, number + 1)
                hi = {"xT": xT_hi, "q": qT_hi, "v": v_hi}[kind]
                act.copy(at(hi, par, slice(CW * h, CW * h + CW)), work_ps[:, bank, :]).then_inc(hi_ready, 1)
                if by_pool((kind, h)) and not (isinstance(b, int) and b == 0):
                    act.copy(whole[:, prologue.index((kind, h)), :], work_ps[:, bank, :]).then_inc(work_copied, 1)

            def exponentials(b, i):
                act.wait_ge(biased_ready, TB * b + i + 1)
                n = P * (i + 1)
                act.activation(probs[:, i % 2, 0:n], biased[:, i % 2, 0:n], ACT.Exp, bias=neg_max[:, i:i + 1],
                               scale=-1.0, accum_out=prob_sum[:, i:i + 1]).then_inc(probs_ready, 1)

            def scale_sum(b, i):
                t = TB * b + i
                act.wait_ge(probs_ready, t + 1)
                act.activation(scaled_sum[:, i:i + 1], prob_sum[:, i:i + 1], ACT.Copy, scale=wpow_inv[:, 1:2])\
                   .then_inc(scaled_ready, 1)

            def copy_probsT(b, i):
                for h in range(i // CT + 1):
                    bank, number = probs_place(b, i, h)
                    n = P * min(CT, i + 1 - CT * h)
                    act.wait_ge(work_filled, number + 1)
                    act.copy(probsT_hi[:, i % 2, CW * h:CW * h + n], work_ps[:, bank, 0:n]).then_inc(probsT_hi_ready, 1)

            def around(b, par, nxt, final):
                for i in range(TB):
                    scale_sum(b, i)
                    if final and i == TB - 1:
                        act.activation(warm[:, :], norm_const[:, 0:1], ACT.Silu)
                    if i + 2 < TB:
                        exponentials(b, i + 2)
                    elif not final:
                        exponentials(b + 1, i + 2 - TB)
                    if i + 1 < TB:
                        copy_probsT(b, i + 1)
                    elif not final:
                        copy_probsT(b + 1, 0)
                    for part in parts_at(i, final):
                        copy_high(b + 1, nxt, *part)

            act.wait_ge(const_ready, N_CONST)
            act.activation(warm[:, :], norm_const[:, 0:1], ACT.Exp)
            act.wait_ge(ffn_w_loaded, 48)
            act.copy(wgu_in[:, :, :], wgu_int[:, :, :]).then_inc(ffn_w_float, 1)
            act.copy(wd_in[:, :], wd_int[:, :]).then_inc(ffn_w_float, 1)
            act.wait_ge(ffn_w_turned, 1)
            gu_f, gu_hi = wguT_f[:, :, :].rearrange("p a n -> p (a n)"), wguT[:, 0, :, :].rearrange("p a n -> p (a n)")
            d_f, d_hi = wdT_f[:, :], wdT[:, 0, :, :].rearrange("p a n -> p (a n)")
            for g in range(2):
                act.copy(gu_f[:, HID * g:HID * (g + 1)], gate_up_w_ps[g]).then_inc(ffn_w_copied, 1)
            act.copy(d_f, down_w_ps).then_inc(ffn_w_copied, 1)
            for part in prologue[:2]:
                copy_high(0, 0, *part)
            act.wait_ge(int_scale_ready, 1)
            act.wait_ge(ffn_w_copied, 3)
            act.activation(gu_f, gu_f, ACT.Copy, scale=int_scale[:, 0:1]).then_inc(ffn_w_scaled, 1)
            copy_high(0, 0, *prologue[2])
            act.activation(d_f, d_f, ACT.Copy, scale=int_scale[:, 1:2]).then_inc(ffn_w_scaled, 1)
            copy_high(0, 0, *prologue[3])
            act.wait_ge(ffn_w_scaled, 1)
            act.copy(gu_hi, gu_f)
            exponentials(0, 0)
            copy_high(0, 0, *prologue[4])
            exponentials(0, 1)
            copy_high(0, 0, *prologue[5])
            copy_probsT(0, 0)
            act.wait_ge(ffn_w_scaled, 2)
            act.copy(d_hi, d_f).then_inc(ffn_w_hi_ready, 1)
            with act.Fori(0, B - 1) as b:
                around(b, act.snap(b % 2), act.snap((b + 1) % 2), False)
            around(B - 1, (B - 1) % 2, B % 2, True)

            def copy_x2_high(c, par):
                act.wait_ge(x2T_filled, c - 1)
                act.copy(x2T_hi[:, par, :], x2T_ps).then_inc(x2T_hi_ready, 1)

            def silus(c, par, blocks=range(HB)):
                for j in blocks:
                    act.wait_ge(gate_up_ready, HB * c + j + 1)
                    act.activation(silu[:, par, j, :], gate_ps[j], ACT.Silu, scale=gate_scale[:, 0:1])\
                       .then_inc(silu_ready, 1)

            def hidden_high(c, par, blocks=range(HB)):
                for j in blocks:
                    act.wait_ge(hidden_ready, HB * c + j + 1)
                    act.copy(hidden_hi[:, par, j, :], hidden[:, par, j, :]).then_inc(hidden_hi_ready, 1)

            def pair(c, final):
                for par in range(2):
                    if final and par == 1:
                        silus(c + par, par, range(HB - 1))
                        hidden_high(c + par, par, range(1))
                        silus(c + par, par, range(HB - 1, HB))
                        hidden_high(c + par, par, range(1, HB))
                        return
                    silus(c + par, par)
                    if not final:
                        copy_x2_high(c + par + 2, par)
                    hidden_high(c + par, par)

            with act.Fori(0, NCH // 2 - 1) as m:
                pair(2 * m, False)
            pair(NCH - 2, True)


_INS = ['L0_attn_x', 'L0_attn_W_qk', 'L0_attn_W_v', 'L0_attn_alibi_slope', 'L0_ffn_w_gate', 'L0_ffn_w_up', 'L0_ffn_w_down']


def kernel(**inputs):
    import numpy as _np
    import concourse.bacc as _bacc
    from concourse import mybir as _mybir
    from concourse.bass_utils import run_bass_kernel_spmd as _run

    nc = _bacc.Bacc("TRN2", target_bir_lowering=False, num_devices=1)
    arrays, args = {}, []
    for name in _INS:
        a = _np.ascontiguousarray(inputs[name])
        arrays[f"in_{name}_dram"] = a
        args.append(nc.dram_tensor(f"in_{name}_dram", a.shape, _mybir.dt.from_np(a.dtype), kind="ExternalInput").ap())
    shape = inputs['L0_attn_x'].shape
    args.append(nc.dram_tensor("out_0_dram", shape, _mybir.dt.float32, kind="ExternalOutput").ap())
    preln_block(nc, *args)
    r = _run(nc, [arrays], core_ids=[0])
    return r.results[0]["out_0_dram"]
```
